# Optimizing a Trainium2 kernel written in Bass

```python
import numpy as np
import jax
import jax.numpy as jnp

def _softmax(x, axis=-1):
    return jax.nn.softmax(x, axis=axis)

def _gelu(x):
    return jax.nn.gelu(x, approximate=True)

def _silu(x):
    return jax.nn.silu(x)

def _sigmoid(x):
    return jax.nn.sigmoid(x)

def _layernorm(x, axis=-1, eps=1e-05):
    m = jnp.mean(x, axis=axis, keepdims=True)
    v = jnp.var(x, axis=axis, keepdims=True)
    return (x - m) / jnp.sqrt(v + eps)

def _scatter_add(tgt, idx, src, axis=0):
    return tgt.at[idx].add(src)

def _segment_sum(src, seg, n):
    return jax.ops.segment_sum(src, seg, n)
kernel_name = 'mk_gnn_preln_d2_gnn_r32_bb5b62'

def setup_inputs(seed: int=0):
    np.random.seed(seed)
    _w = jnp.asarray

    def _rec_inputs():
        import jax
        import jax.numpy as jnp
        _gk = jax.random.key(seed)
        x = -0.0005121 + 1.001 * jax.random.normal(jax.random.fold_in(_gk, 1), (3125, 160), jnp.float32)
        src = jax.random.randint(jax.random.fold_in(_gk, 2), (100000,), 0, 3125, jnp.int32)
        dst = jax.random.randint(jax.random.fold_in(_gk, 3), (100000,), 0, 3125, jnp.int32)
        _o = jnp.argsort(dst, stable=True)
        src = src[_o]
        dst = dst[_o]
        edge_attr_16 = jax.random.uniform(jax.random.fold_in(_gk, 12), (100000, 16), jnp.float32, 0.0, 1)
        edge_attr_4 = 0.000898722 + 1.00012 * jax.random.normal(jax.random.fold_in(_gk, 13), (100000, 4), jnp.float32)
        edge_attr_64 = 0.000127647 + 1.00004 * jax.random.normal(jax.random.fold_in(_gk, 14), (100000, 64), jnp.float32)
        node_vec1 = jax.random.uniform(jax.random.fold_in(_gk, 16), (3125, 1), jnp.float32, 0.0, 1)
        return (x, src, dst, edge_attr_16, edge_attr_4, edge_attr_64, node_vec1)
    x, src, dst, edge_attr_16, edge_attr_4, edge_attr_64, node_vec1 = _rec_inputs()

    def _L0_gnn_setup():
        import jax, jax.numpy as jnp
        import numpy as np
        N, E = (625, 10000)
        CS, CV = (64, 32)
        AS_, AV, H = (16, 8, 4)
        NB = 16
        SQRT3 = 1.7320508075688772
        SQRT2 = 1.4142135623730951
        EPS = 1e-05

        def _cg_tp(s, v, y0, y1, w_ss, w_sv, w_vs, w_vv0, w_vv1):
            out_s = jnp.concatenate([w_ss * s * y0[:, None], w_vv0 * (jnp.einsum('eci,ei->ec', v, y1) / SQRT3)], axis=-1)
            out_v = jnp.concatenate([(w_sv * s)[:, :, None] * y1[:, None, :], (w_vs * jnp.ones_like(v[..., 0]))[..., None] * v * y0[:, None, None], (w_vv1 * jnp.ones_like(v[..., 0]))[..., None] * (jnp.cross(v, y1[:, None, :]) / SQRT2)], axis=1)
            return (out_s, out_v)

        def _equiv_layernorm(s, v, gamma_s, beta_s, gamma_v):
            mu = jnp.mean(s, axis=-1, keepdims=True)
            var = jnp.var(s, axis=-1, keepdims=True)
            s_n = (s - mu) * jax.lax.rsqrt(var + EPS) * gamma_s + beta_s
            rms = jnp.sqrt(jnp.mean(jnp.sum(v * v, axis=-1), axis=-1, keepdims=True) + EPS)
            v_n = v / rms[..., None] * gamma_v[None, :, None]
            return (s_n, v_n)
        key = jax.random.key(seed)
        ks = jax.random.split(key, 26)

        def rn(k, shape, fan):
            return jax.random.normal(k, shape, jnp.float32) / np.sqrt(fan)
        D1S, D1V = (CS + CV, CS + 2 * CV)
        WN = 2 * CS + 3 * CV
        inp = {'node': jax.random.normal(ks[0], (N, CS + 3 * CV), jnp.float32), 'edge_index': jax.random.randint(ks[1], (2, E), 0, N, jnp.int64 if jax.config.jax_enable_x64 else jnp.int32), 'rbf': jax.random.uniform(ks[2], (E, NB), jnp.float32), 'rsh': jax.random.normal(ks[3], (E, 4), jnp.float32), 'gamma_s': jnp.ones((CS,), jnp.float32), 'beta_s': jnp.zeros((CS,), jnp.float32), 'gamma_v': jnp.ones((CV,), jnp.float32), 'Ws_src': rn(ks[4], (CS, CS), CS), 'Wv_src': rn(ks[5], (CV, CV), CV), 'Ws_dst': rn(ks[6], (CS, CS), CS), 'Wv_dst': rn(ks[7], (CV, CV), CV), 'W_rbf': rn(ks[8], (NB, WN), NB), 'W_alpha': rn(ks[9], (D1S, H * AS_), D1S), 'alpha_dot': rn(ks[10], (1, H, AS_), AS_), 'Ws_val': rn(ks[11], (D1S, CS), D1S), 'Wv_val': rn(ks[12], (D1V, CV), D1V), 'Wg': rn(ks[13], (CS, CV), CS), 'w2_ss': rn(ks[14], (CS,), 1), 'w2_sv': rn(ks[15], (CS,), 1), 'w2_vs': rn(ks[16], (CV,), 1), 'w2_vv0': rn(ks[17], (CV,), 1), 'w2_vv1': rn(ks[18], (CV,), 1), 'Ws_vlin': rn(ks[19], (D1S, H * AS_), D1S), 'Wv_vlin': rn(ks[20], (D1V, H * AV), D1V), 'Wps': rn(ks[21], (H * AS_, CS), H * AS_), 'Wpv': rn(ks[22], (H * AV, CV), H * AV)}
        return inp
    _L0_gnn_all = _L0_gnn_setup()
    _L0_gnn_in = {k: v for k, v in _L0_gnn_all.items() if k in ('gamma_s', 'beta_s', 'gamma_v', 'Ws_src', 'Wv_src', 'Ws_dst', 'Wv_dst', 'W_rbf', 'W_alpha', 'alpha_dot', 'Ws_val', 'Wv_val', 'Wg', 'w2_ss', 'w2_sv', 'w2_vs', 'w2_vv0', 'w2_vv1', 'Ws_vlin', 'Wv_vlin', 'Wps', 'Wpv')}
    del _L0_gnn_all

    def _L1_gnn_setup():
        import jax, jax.numpy as jnp
        import numpy as np
        N, E = (1250, 20000)
        S_IN, V_IN = (64, 32)
        S_MID, V_MID = (96, 128)
        S_OUT, V_OUT = (96, 32)
        R = 64
        FC_HID = 64
        W_NUMEL = 64 + 64 + 32 + 32 + 32
        NUM_NEIGHBORS = 16.0

        def _inv(d):
            return 1.0 / jnp.sqrt(jnp.float32(d))

        def _forward(node_features, node_attr, edge_attr, edge_scalars, lin1_ws, lin1_wv, fc_w1, fc_w2, sc_ws, sc_wv, lin2_ws, lin2_wv, edge_src, edge_dst):
            n = node_features.shape[0]
            s = node_features[:, :S_IN]
            v = node_features[:, S_IN:].reshape(n, V_IN, 3)
            a = node_attr
            sc_s = s @ sc_ws * a * _inv(S_IN)
            sc_v = jnp.einsum('nci,cd->ndi', v, sc_wv) * a[:, :, None] * _inv(V_IN)
            h_s = s @ lin1_ws * a * _inv(S_IN)
            h_v = jnp.einsum('nci,cd->ndi', v, lin1_wv) * a[:, :, None] * _inv(V_IN)
            hid = jax.nn.silu(edge_scalars @ fc_w1 * _inv(R))
            w = hid @ fc_w2 * _inv(FC_HID)
            w1, w2, w3, w4, w5 = jnp.split(w, [64, 128, 160, 192], axis=-1)
            es = h_s[edge_src]
            ev = h_v[edge_src]
            e0 = edge_attr[:, :1]
            e1 = edge_attr[:, 1:4]
            m_s1 = w1 * es * e0
            m_s2 = w4 * jnp.einsum('eci,ei->ec', ev, e1) * _inv(3)
            m_v1 = (w2 * es)[:, :, None] * e1[:, None, :]
            m_v2 = w3[:, :, None] * ev * e0[:, :, None]
            m_v3 = w5[:, :, None] * jnp.cross(ev, e1[:, None, :]) * _inv(2)
            mid_s = jnp.concatenate([m_s1, m_s2], axis=-1)
            mid_v = jnp.concatenate([m_v1, m_v2, m_v3], axis=1)
            inv_nn = 1.0 / jnp.sqrt(jnp.float32(NUM_NEIGHBORS))
            agg_s = jax.ops.segment_sum(mid_s, edge_dst, num_segments=n) * inv_nn
            agg_v = jax.ops.segment_sum(mid_v, edge_dst, num_segments=n) * inv_nn
            o_s = agg_s @ lin2_ws * a * _inv(S_MID)
            o_v = jnp.einsum('nci,cd->ndi', agg_v, lin2_wv) * a[:, :, None] * _inv(V_MID)
            pre_s = sc_s + o_s
            pre_v = sc_v + o_v
            scalars = jax.nn.silu(pre_s[:, :64])
            gates = jax.nn.sigmoid(pre_s[:, 64:96])
            gated = gates[:, :, None] * pre_v
            return jnp.concatenate([scalars, gated.reshape(n, 3 * V_OUT)], axis=-1)
        key = jax.random.key(seed)
        ks = jax.random.split(key, 13)
        return {'node_features': jax.random.normal(ks[0], (N, S_IN + 3 * V_IN), jnp.float32), 'node_attr': jnp.ones((N, 1), jnp.float32), 'edge_src': jax.random.randint(ks[1], (E,), 0, N), 'edge_dst': jax.random.randint(ks[2], (E,), 0, N), 'edge_attr': jax.random.normal(ks[3], (E, 4), jnp.float32), 'edge_scalars': jax.random.normal(ks[4], (E, R), jnp.float32), 'lin1_ws': jax.random.normal(ks[5], (S_IN, S_IN), jnp.float32), 'lin1_wv': jax.random.normal(ks[6], (V_IN, V_IN), jnp.float32), 'fc_w1': jax.random.normal(ks[7], (R, FC_HID), jnp.float32), 'fc_w2': jax.random.normal(ks[8], (FC_HID, W_NUMEL), jnp.float32), 'sc_ws': jax.random.normal(ks[9], (S_IN, S_OUT), jnp.float32), 'sc_wv': jax.random.normal(ks[10], (V_IN, V_OUT), jnp.float32), 'lin2_ws': jax.random.normal(ks[11], (S_MID, S_OUT), jnp.float32), 'lin2_wv': jax.random.normal(ks[12], (V_MID, V_OUT), jnp.float32)}
    _L1_gnn_all = _L1_gnn_setup()
    _L1_gnn_in = {k: v for k, v in _L1_gnn_all.items() if k in ('lin1_ws', 'lin1_wv', 'fc_w1', 'fc_w2', 'sc_ws', 'sc_wv', 'lin2_ws', 'lin2_wv')}
    del _L1_gnn_all
    return {'x': x, 'src': src, 'dst': dst, 'edge_attr_16': edge_attr_16, 'edge_attr_4': edge_attr_4, 'edge_attr_64': edge_attr_64, 'node_vec1': node_vec1, 'L0_gnn_gamma_s': _L0_gnn_in['gamma_s'], 'L0_gnn_beta_s': _L0_gnn_in['beta_s'], 'L0_gnn_gamma_v': _L0_gnn_in['gamma_v'], 'L0_gnn_Ws_src': _L0_gnn_in['Ws_src'], 'L0_gnn_Wv_src': _L0_gnn_in['Wv_src'], 'L0_gnn_Ws_dst': _L0_gnn_in['Ws_dst'], 'L0_gnn_Wv_dst': _L0_gnn_in['Wv_dst'], 'L0_gnn_W_rbf': _L0_gnn_in['W_rbf'], 'L0_gnn_W_alpha': _L0_gnn_in['W_alpha'], 'L0_gnn_alpha_dot': _L0_gnn_in['alpha_dot'], 'L0_gnn_Ws_val': _L0_gnn_in['Ws_val'], 'L0_gnn_Wv_val': _L0_gnn_in['Wv_val'], 'L0_gnn_Wg': _L0_gnn_in['Wg'], 'L0_gnn_w2_ss': _L0_gnn_in['w2_ss'], 'L0_gnn_w2_sv': _L0_gnn_in['w2_sv'], 'L0_gnn_w2_vs': _L0_gnn_in['w2_vs'], 'L0_gnn_w2_vv0': _L0_gnn_in['w2_vv0'], 'L0_gnn_w2_vv1': _L0_gnn_in['w2_vv1'], 'L0_gnn_Ws_vlin': _L0_gnn_in['Ws_vlin'], 'L0_gnn_Wv_vlin': _L0_gnn_in['Wv_vlin'], 'L0_gnn_Wps': _L0_gnn_in['Wps'], 'L0_gnn_Wpv': _L0_gnn_in['Wpv'], 'L1_gnn_lin1_ws': _L1_gnn_in['lin1_ws'], 'L1_gnn_lin1_wv': _L1_gnn_in['lin1_wv'], 'L1_gnn_fc_w1': _L1_gnn_in['fc_w1'], 'L1_gnn_fc_w2': _L1_gnn_in['fc_w2'], 'L1_gnn_sc_ws': _L1_gnn_in['sc_ws'], 'L1_gnn_sc_wv': _L1_gnn_in['sc_wv'], 'L1_gnn_lin2_ws': _L1_gnn_in['lin2_ws'], 'L1_gnn_lin2_wv': _L1_gnn_in['lin2_wv']}

def reference(x, src, dst, edge_attr_16, edge_attr_4, edge_attr_64, node_vec1, L0_gnn_gamma_s, L0_gnn_beta_s, L0_gnn_gamma_v, L0_gnn_Ws_src, L0_gnn_Wv_src, L0_gnn_Ws_dst, L0_gnn_Wv_dst, L0_gnn_W_rbf, L0_gnn_W_alpha, L0_gnn_alpha_dot, L0_gnn_Ws_val, L0_gnn_Wv_val, L0_gnn_Wg, L0_gnn_w2_ss, L0_gnn_w2_sv, L0_gnn_w2_vs, L0_gnn_w2_vv0, L0_gnn_w2_vv1, L0_gnn_Ws_vlin, L0_gnn_Wv_vlin, L0_gnn_Wps, L0_gnn_Wpv, L1_gnn_lin1_ws, L1_gnn_lin1_wv, L1_gnn_fc_w1, L1_gnn_fc_w2, L1_gnn_sc_ws, L1_gnn_sc_wv, L1_gnn_lin2_ws, L1_gnn_lin2_wv):
    import jax
    import jax.numpy as jnp

    def _L0_gnn_ref(node, rbf, rsh, gamma_s, beta_s, gamma_v, Ws_src, Wv_src, Ws_dst, Wv_dst, W_rbf, W_alpha, alpha_dot, Ws_val, Wv_val, Wg, w2_ss, w2_sv, w2_vs, w2_vv0, w2_vv1, Ws_vlin, Wv_vlin, Wps, Wpv, edge_index):
        import jax, jax.numpy as jnp
        import numpy as np
        N, E = (625, 10000)
        CS, CV = (64, 32)
        AS_, AV, H = (16, 8, 4)
        NB = 16
        SQRT3 = 1.7320508075688772
        SQRT2 = 1.4142135623730951
        EPS = 1e-05

        def _cg_tp(s, v, y0, y1, w_ss, w_sv, w_vs, w_vv0, w_vv1):
            out_s = jnp.concatenate([w_ss * s * y0[:, None], w_vv0 * (jnp.einsum('eci,ei->ec', v, y1) / SQRT3)], axis=-1)
            out_v = jnp.concatenate([(w_sv * s)[:, :, None] * y1[:, None, :], (w_vs * jnp.ones_like(v[..., 0]))[..., None] * v * y0[:, None, None], (w_vv1 * jnp.ones_like(v[..., 0]))[..., None] * (jnp.cross(v, y1[:, None, :]) / SQRT2)], axis=1)
            return (out_s, out_v)

        def _equiv_layernorm(s, v, gamma_s, beta_s, gamma_v):
            mu = jnp.mean(s, axis=-1, keepdims=True)
            var = jnp.var(s, axis=-1, keepdims=True)
            s_n = (s - mu) * jax.lax.rsqrt(var + EPS) * gamma_s + beta_s
            rms = jnp.sqrt(jnp.mean(jnp.sum(v * v, axis=-1), axis=-1, keepdims=True) + EPS)
            v_n = v / rms[..., None] * gamma_v[None, :, None]
            return (s_n, v_n)
        n = node.shape[0]
        e = rsh.shape[0]
        s = node[:, :CS]
        v = node[:, CS:].reshape(n, CV, 3)
        s_n, v_n = _equiv_layernorm(s, v, gamma_s, beta_s, gamma_v)
        src, dst = (edge_index[0], edge_index[1])
        msg_s = (s_n @ Ws_src)[src] + (s_n @ Ws_dst)[dst]
        msg_v = jnp.einsum('ncx,cd->ndx', v_n, Wv_src)[src] + jnp.einsum('ncx,cd->ndx', v_n, Wv_dst)[dst]
        y0, y1 = (rsh[:, 0], rsh[:, 1:4])
        w1 = rbf @ W_rbf
        m1_s, m1_v = _cg_tp(msg_s, msg_v, y0, y1, w1[:, :CS], w1[:, CS:2 * CS], w1[:, 2 * CS:2 * CS + CV], w1[:, 2 * CS + CV:2 * CS + 2 * CV], w1[:, 2 * CS + 2 * CV:])
        a = (m1_s @ W_alpha).reshape(e, H, AS_)
        a = jnp.where(a > 0, a, 0.2 * a)
        a = jnp.sum(a * alpha_dot, axis=-1, keepdims=True)
        amax = jax.ops.segment_max(a, dst, num_segments=n)
        amax = jnp.where(jnp.isfinite(amax), amax, 0.0)
        ex = jnp.exp(a - amax[dst])
        den = jax.ops.segment_sum(ex, dst, num_segments=n)
        alpha = ex / (den[dst] + 1e-16)
        val_s = m1_s @ Ws_val
        val_v = jnp.einsum('ecx,cd->edx', m1_v, Wv_val)
        val_v = val_v * jax.nn.sigmoid(val_s @ Wg)[..., None]
        val_s = jax.nn.sigmoid(val_s)
        m2_s, m2_v = _cg_tp(val_s, val_v, y0, y1, w2_ss, w2_sv, w2_vs, w2_vv0, w2_vv1)
        hs = (m2_s @ Ws_vlin).reshape(e, H, AS_)
        hv = jnp.einsum('ecx,cd->edx', m2_v, Wv_vlin).reshape(e, H, AV, 3)
        h = jnp.concatenate([hs, hv.reshape(e, H, AV * 3)], axis=-1)
        agg = jax.ops.segment_sum(alpha * h, dst, num_segments=n)
        agg_s = agg[:, :, :AS_].reshape(n, H * AS_)
        agg_v = agg[:, :, AS_:].reshape(n, H * AV, 3)
        out = node + jnp.concatenate([agg_s @ Wps, jnp.einsum('ncx,cd->ndx', agg_v, Wpv).reshape(n, CV * 3)], axis=-1)
        return out

    def _L1_gnn_ref(node_features, node_attr, edge_src, edge_dst, edge_attr, edge_scalars, lin1_ws, lin1_wv, fc_w1, fc_w2, sc_ws, sc_wv, lin2_ws, lin2_wv):
        import jax, jax.numpy as jnp
        import numpy as np
        N, E = (1250, 20000)
        S_IN, V_IN = (64, 32)
        S_MID, V_MID = (96, 128)
        S_OUT, V_OUT = (96, 32)
        R = 64
        FC_HID = 64
        W_NUMEL = 64 + 64 + 32 + 32 + 32
        NUM_NEIGHBORS = 16.0

        def _inv(d):
            return 1.0 / jnp.sqrt(jnp.float32(d))

        def _forward(node_features, node_attr, edge_attr, edge_scalars, lin1_ws, lin1_wv, fc_w1, fc_w2, sc_ws, sc_wv, lin2_ws, lin2_wv, edge_src, edge_dst):
            n = node_features.shape[0]
            s = node_features[:, :S_IN]
            v = node_features[:, S_IN:].reshape(n, V_IN, 3)
            a = node_attr
            sc_s = s @ sc_ws * a * _inv(S_IN)
            sc_v = jnp.einsum('nci,cd->ndi', v, sc_wv) * a[:, :, None] * _inv(V_IN)
            h_s = s @ lin1_ws * a * _inv(S_IN)
            h_v = jnp.einsum('nci,cd->ndi', v, lin1_wv) * a[:, :, None] * _inv(V_IN)
            hid = jax.nn.silu(edge_scalars @ fc_w1 * _inv(R))
            w = hid @ fc_w2 * _inv(FC_HID)
            w1, w2, w3, w4, w5 = jnp.split(w, [64, 128, 160, 192], axis=-1)
            es = h_s[edge_src]
            ev = h_v[edge_src]
            e0 = edge_attr[:, :1]
            e1 = edge_attr[:, 1:4]
            m_s1 = w1 * es * e0
            m_s2 = w4 * jnp.einsum('eci,ei->ec', ev, e1) * _inv(3)
            m_v1 = (w2 * es)[:, :, None] * e1[:, None, :]
            m_v2 = w3[:, :, None] * ev * e0[:, :, None]
            m_v3 = w5[:, :, None] * jnp.cross(ev, e1[:, None, :]) * _inv(2)
            mid_s = jnp.concatenate([m_s1, m_s2], axis=-1)
            mid_v = jnp.concatenate([m_v1, m_v2, m_v3], axis=1)
            inv_nn = 1.0 / jnp.sqrt(jnp.float32(NUM_NEIGHBORS))
            agg_s = jax.ops.segment_sum(mid_s, edge_dst, num_segments=n) * inv_nn
            agg_v = jax.ops.segment_sum(mid_v, edge_dst, num_segments=n) * inv_nn
            o_s = agg_s @ lin2_ws * a * _inv(S_MID)
            o_v = jnp.einsum('nci,cd->ndi', agg_v, lin2_wv) * a[:, :, None] * _inv(V_MID)
            pre_s = sc_s + o_s
            pre_v = sc_v + o_v
            scalars = jax.nn.silu(pre_s[:, :64])
            gates = jax.nn.sigmoid(pre_s[:, 64:96])
            gated = gates[:, :, None] * pre_v
            return jnp.concatenate([scalars, gated.reshape(n, 3 * V_OUT)], axis=-1)
        return _forward(node_features, node_attr, edge_attr, edge_scalars, lin1_ws, lin1_wv, fc_w1, fc_w2, sc_ws, sc_wv, lin2_ws, lin2_wv, edge_src, edge_dst)
    edge_index = jnp.stack([src, dst])
    h = jnp.maximum(_layernorm(x, axis=-1), 0.0)
    x = x + _L0_gnn_ref(h, edge_attr_16, edge_attr_4, L0_gnn_gamma_s, L0_gnn_beta_s, L0_gnn_gamma_v, L0_gnn_Ws_src, L0_gnn_Wv_src, L0_gnn_Ws_dst, L0_gnn_Wv_dst, L0_gnn_W_rbf, L0_gnn_W_alpha, L0_gnn_alpha_dot, L0_gnn_Ws_val, L0_gnn_Wv_val, L0_gnn_Wg, L0_gnn_w2_ss, L0_gnn_w2_sv, L0_gnn_w2_vs, L0_gnn_w2_vv0, L0_gnn_w2_vv1, L0_gnn_Ws_vlin, L0_gnn_Wv_vlin, L0_gnn_Wps, L0_gnn_Wpv, edge_index)
    h = jnp.maximum(_layernorm(x, axis=-1), 0.0)
    x = x + _L1_gnn_ref(h, node_vec1, src, dst, edge_attr_4, edge_attr_64, L1_gnn_lin1_ws, L1_gnn_lin1_wv, L1_gnn_fc_w1, L1_gnn_fc_w2, L1_gnn_sc_ws, L1_gnn_sc_wv, L1_gnn_lin2_ws, L1_gnn_lin2_wv)
    return x

_drawn_inputs = setup_inputs


def setup_inputs(seed=0):
    import zlib

    import numpy as np

    out = dict(_drawn_inputs(seed))
    spreads = {'L0_gnn_gamma_s': (1.0, 0.6), 'L0_gnn_beta_s': (0.0, 0.8), 'L0_gnn_gamma_v': (1.0, 0.6)}
    factors = {'L0_gnn_w2_vv1': 2.987}
    for name, (base, spread) in spreads.items():
        noise = np.random.default_rng([zlib.crc32(name.encode()), seed]).standard_normal(out[name].shape)
        drawn = base * np.exp(spread * noise) if base else spread * noise
        out[name] = jnp.asarray(drawn.astype(out[name].dtype))
    for name, factor in factors.items():
        out[name] = (out[name] * factor).astype(out[name].dtype)
    return out
```

```python
from contextlib import ExitStack

import numpy as np
import concourse.bass as bass
from concourse import mybir

F32 = mybir.dt.float32
I32 = mybir.dt.int32
ALU = mybir.AluOpType
ACT = mybir.ActivationFunctionType
AX = mybir.AxisListType

P = 128
N = 3125
NT = -(-N // P)
NP = NT * P
E = 100000
G = 2
CH = G * P
U = 4
NCH = 392
EP = NCH * CH
VS = NCH + NT - 1
S = 64
C = 32
D = S + 3 * C
H = 4
HW = D // H + 1
MW = 96 + 3 * 128
EPS = 1e-5
NEG = -1e30
R2, R3 = 2.0 ** -0.5, 3.0 ** -0.5
assert VS % U == 0 and NCH * CH >= E


def ax(ap, *dims):
    return bass.AP(ap.tensor, ap.offset, [list(ap.ap[0])] + [list(d) for d in dims])


class Chain:

    def __init__(self, eng, sem):
        self.eng, self.sem, self.n = eng, sem, 0

    def add(self, ins):
        self.n += 1
        return ins.then_inc(self.sem, 1)

    def wait(self):
        self.eng.wait_ge(self.sem, self.n)

    def step(self, ins):
        self.add(ins)
        self.wait()

    def restart(self):
        self.wait()
        self.eng.sem_clear(self.sem)
        self.n = 0


class Visit:

    def __init__(self, first, base=None, table=None):
        self.first, self.base, self.table = first, base, table
        self.slot = first % U
        self.par = first % 2

    def __add__(self, d):
        return Visit(self.first + d, self.base, self.table)

    @property
    def num(self):
        return self.first if self.base is None else self.base + self.first

    def round(self, per):
        if self.base is None:
            return per * (self.first // U + 1)
        return self.base * (per // U) + per * (self.first // U + 1)

    def chunk(self, eng):
        if self.table is None:
            return self.num // NT
        return eng.value_load(self.table[0:1, 0, bass.ds(self.num, 1)], min_val=0, max_val=NCH - 1)

    def node_tile(self, eng):
        if self.table is None:
            return self.num % NT
        return eng.value_load(self.table[0:1, 1, bass.ds(self.num, 1)], min_val=0, max_val=NT - 1)

    def reused(self):
        return self.base is not None or self.first >= U


VG = NCH * NT
assert VG % U == 0


def program(nc, a, out):
    ctx = ExitStack()
    with ctx:
        def sb(name, shape, dt=F32):
            return ctx.enter_context(nc.sbuf_tensor(name, shape, dt))

        def ps(name, shape):
            return ctx.enter_context(nc.psum_tensor(name, shape, F32))

        def sem(name):
            return ctx.enter_context(nc.semaphore(name))

        src_tab = nc.dram_tensor("src_tab", [NP, D], F32)
        hid_tab = nc.dram_tensor("hid_tab", [NP, D], F32)
        vis_tab = nc.dram_tensor("vis_tab", [2, U * P], I32)

        ident = sb("ident", [P, P])
        iota = sb("iota", [P, P])
        nodecon = sb("nodecon", [P, NT, 2])
        vcol = sb("vcol", [P, U])
        tplus = sb("tplus", [1, NCH])
        ones = sb("ones", [1, P])
        w_edge0 = sb("w_edge0", [64, MW])
        w_ms0 = sb("w_ms0", [96, 160])
        w_mv0 = sb("w_mv0", [P, C])
        w_hs0 = sb("w_hs0", [96, S])
        w_hv0 = sb("w_hv0", [P, C])
        w2s = sb("w2s", [96, 1])
        w2v = sb("w2v", [P, 1])
        ws_val_t = sb("ws_val_t", [S, 96])
        wg = sb("wg", [S, C])
        adot = sb("adot", [P, S])
        gam_s = sb("gam_s", [S, 1])
        bet_s = sb("bet_s", [S, 1])
        gam_v = sb("gam_v", [96, 1])
        n0s = sb("n0s", [S, 2 * S])
        n0v = sb("n0v", [96, 192])
        e0s = sb("e0s", [S, S])
        e0v = sb("e0v", [96, 96])
        n1s = sb("n1s", [S, 160])
        n1v = sb("n1v", [96, 192])
        fc1 = sb("fc1", [64, P])
        w_edge1 = sb("w_edge1", [P, MW])
        l2s = sb("l2s", [96, 96])
        l2v = sb("l2v", [P, C])
        attr = sb("attr", [P, NT])

        X = sb("X", [P, NT, D])
        HN = sb("HN", [P, NT, D])
        TAB = sb("TAB", [P, NT, D])
        SC = sb("SC", [P, NT, 192])
        XN = SC[:, :, :].rearrange("p j f -> p (j f)")[:, 0:NT * D].rearrange("p (j f) -> p j f", j=NT)
        ACC = sb("ACC", [P, NT, MW])
        m_run = sb("m_run", [P, NT, H])
        st = sb("st", [P, 6, NT])
        accA = ACC[:, :, :].rearrange("p j f -> p (j f)")[:, 0:NT * H * HW].rearrange("p (j f) -> p j f", j=NT)
        DT = ACC[:, :, :].rearrange("p j f -> p (j f)")[:, NT * H * HW:NT * (H * HW + D)]\
            .rearrange("p (j f) -> p j f", j=NT)
        tr_n = sb("tr_n", [P, 4, P])
        o_n = sb("o_n", [P, 192])

        last = sb("last", [1, NCH], I32)
        lastf = sb("lastf", [1, NCH])
        spare = SC[:, :, :].rearrange("p j f -> p (j f)")[:, NT * D:NT * 192]
        bound, cmpv = spare[:, 0:NCH], spare[:, NCH:2 * NCH]
        tcol = sb("tcol", [P, 2, U])
        tcoli = sb("tcoli", [P, 2, U], I32)
        flag = sb("flag", [1, 1], I32)
        dstw = TAB[:, :, :].rearrange("p j f -> p (j f)")[:, 0:EP // P + 1].bitcast(I32)
        down = HN[:, :, :].rearrange("p j f -> p (j f)")[:, 0:EP // P + 1]
        onec = sb("onec", [P, 1])
        vis = sb("vis", [1, 2, U * P], I32)

        sd = sb("sd", [P, U, 2 * G], I32)
        ncol = sb("ncol", [P, U, 2])
        sdf = sb("sdf", [P, U, G])
        drow = sb("drow", [P, U, CH], I32)
        yed = sb("yed", [P, U, G * 4])
        yrep = sb("yrep", [P, U, 2, CH])
        rrep = sb("rrep", [64, U, CH])
        zt = sb("zt", [64, U, CH])
        gat = sb("gat", [P, U, G * D])
        ohT = sb("ohT", [P, U, CH])
        ohE = sb("ohE", [P, U, G, P])
        mneg = sb("mneg", [P, U, CH])
        SV = sb("SV", [P, G, D + 64])
        M = sb("M", [P, 2, G, MW])
        row_n = M[:, 0, 0, :]
        tA = sb("tA", [P, G, 3, C])
        tB = sb("tB", [P, G, 3, C])
        tC = sb("tC", [P, G, 3, C])
        tD = sb("tD", [P, G, C])
        MT = sb("MT", [P, 4, G, P])
        MT2 = sb("MT2", [P, 4, G, P])
        M2 = sb("M2", [P, G, MW])
        th = sb("th", [P, 2, G, 96])
        sig = sb("sig", [P, G, 96])
        SV2 = sb("SV2", [P, G, D + 64])
        lk = sb("lk", [P, G, S])
        lk2 = sb("lk2", [P, G, S])
        a4 = sb("a4", [P, U, G, H])
        scr = sb("scr", [P, CH])
        mo = sb("mo", [P, U, H])
        mn = sb("mn", [P, U, H])
        mdf = sb("mdf", [P, U, H])
        cor = sb("cor", [P, U, H])
        ad = sb("ad", [P, G * H])
        ex = sb("ex", [P, G * H])
        HX = sb("HX", [P, G, H, HW])
        atmp = sb("atmp", [P, H, HW])
        hid = MT2[:, 0:2].rearrange("p a g e -> p a (g e)")
        hidy = MT[:, :].rearrange("p (a b) g e -> p a b (g e)", a=2)

        W = ps("W", [P, G, 512])
        TR = ps("TR", [P, 8, P])
        DM = ps("DM", [P, 512])
        E1 = ps("E1", [P, G, 256])
        HP = ps("HP", [P, 512])
        AG = ps("AG", [P, 512])
        W_1 = TR[:, :, :].rearrange("p a b -> p (a b)").rearrange("p (g f) -> p g f", g=G)
        Wr = [W, W_1]

        s_const = sem("s_const")
        s_zero = sem("s_zero")
        s_w = sem("s_w")
        s_prep = sem("s_prep")
        s_wsg = sem("s_wsg")
        s_bnd = sem("s_bnd")
        s_tcol = sem("s_tcol")
        s_vst = sem("s_vst")
        s_vis = sem("s_vis")
        s_passed = sem("s_passed")
        s_dve = sem("s_dve")
        s_pool = sem("s_pool")
        s_act = sem("s_act")
        s_nrm = [sem(f"s_nrm{i}") for i in range(5)]
        s_sq = sem("s_sq")
        s_tab0 = sem("s_tab0")
        s_tab0d = sem("s_tab0d")
        s_tab1 = sem("s_tab1")
        s_tab1d = sem("s_tab1d")
        s_out = sem("s_out")
        s_outd = sem("s_outd")
        nd = {ph: {k: sem(f"{ph}_{k}") for k in ("row", "tr", "cp", "mm", "ev")} for ph in ("n0", "e0", "n1", "fi")}

        def node_tiles(eng, body):
            body(0, True)
            with eng.Fori(1, NT) as j:
                body(j, False)

        def node_pe(pe, ph, feats, mats):
            s = nd[ph]

            def body(j, first):
                if not first:
                    pe.wait_ge(s["cp"], j)
                pe.wait_ge(s["row"], j + 1)
                for b, (lo, w) in enumerate(feats):
                    ins = nc.tensor.transpose(TR[0:w, b, :], row_n[:, lo:lo + w], ident[:, :])
                ins.then_inc(s["tr"], 1)
                pe.wait_ge(s["cp"], j + 1)
                if not first:
                    pe.wait_ge(s["ev"], j)
                for o, lhs, rhs in mats:
                    ins = nc.tensor.matmul(o, lhs, rhs, start=True, stop=True)
                ins.then_inc(s["mm"], 1)
            node_tiles(pe, body)

        def node_act(act, ph, rows, width):
            def body(j, first):
                if not first:
                    act.wait_ge(nd[ph]["tr"], j)
                nc.scalar.activation(row_n[:, 0:width], rows[:, bass.ds(j, 1), :].rearrange("p a f -> p (a f)"),
                                     ACT.Copy).then_inc(nd[ph]["row"], 1)
            node_tiles(act, body)

        def loop_visits(eng, lead, tail, stage, finish=lambda total: None):
            def run(total, table):
                for t in range(-lead, U):
                    stage(Visit(t, None, table), total)
                with eng.Fori(U, total - U, U) as base:
                    for u in range(U):
                        stage(Visit(u, base, table), None)
                for t in range(total - U, total + tail):
                    stage(Visit(t, None, table), total)
                finish(total)

            descents = eng.value_load(flag[0:1, 0:1], min_val=0, max_val=EP)
            with eng.If(descents == 0):
                run(VS, vis)
            with eng.Else():
                run(VG, None)

        def inside(v, total):
            return total is None or 0 <= v.first < total

        LA = dict(ld=[sem(f"a_ld{u}") for u in range(U)], ga=[sem(f"a_ga{u}") for u in range(U)],
                  **{k: sem(f"a_{k}") for k in ("cvt", "z", "oh", "oht", "pre", "msg", "dup", "m", "t1", "c1", "e1", "th", "a4", "ab",
                                     "sv2", "dup2", "m2", "mx", "t2", "c2", "h", "d", "ex", "hx", "exs", "sc", "acc")})
        LB = dict(ld=[sem(f"b_ld{u}") for u in range(U)], ga=[sem(f"b_ga{u}") for u in range(U)],
                  **{k: sem(f"b_{k}") for k in ("cvt", "oh", "fc", "hid", "hy", "w", "dup", "m", "sc", "acc")})

        def products(dve, ch, SVt, w_s0, w_sv, w_vs, w_dot, w_cr, Mt, dup_wait):
            nc.vector.tensor_tensor(Mt[:, :, 0:S], SVt[:, :, 0:S], w_s0, ALU.mult)
            v3 = SVt[:, :, S:D].rearrange("p g (k c) -> p g k c", k=3)
            blocks = Mt[:, :, 96:MW].rearrange("p g (k f) -> p g k f", k=3)
            for g in range(G):
                nc.vector.tensor_tensor(blocks[:, g, :, 0:S], ax(SVt[:, g, 0:S], (0, 3), (1, S)), w_sv(g), ALU.mult)
                nc.vector.tensor_tensor(blocks[:, g, :, S:S + C], v3[:, g], w_vs(g), ALU.mult)
                ch.add(nc.vector.tensor_tensor(tA[:, g], v3[:, g], w_dot(g), ALU.mult))
            dup_wait()
            for g in range(G):
                v5 = SVt[:, g, S:D + 64].rearrange("p (k c) -> p k c", k=5)
                nc.vector.tensor_tensor(tB[:, g], v5[:, 2:5], w_cr(g), ALU.mult)
                ch.add(nc.vector.tensor_tensor(tC[:, g], v5[:, 1:4], w_cr(g), ALU.mult))
            ch.wait()
            ch.add(nc.vector.tensor_tensor(tD[:, :, :], tA[:, :, 0], tA[:, :, 1], ALU.add))
            for k in range(3):
                nc.vector.tensor_tensor(blocks[:, :, k, S + C:], tB[:, :, (k + 2) % 3], tC[:, :, (k + 1) % 3],
                                        ALU.subtract)
            ch.wait()
            return nc.vector.tensor_tensor(Mt[:, :, S:96], tD[:, :, :], tA[:, :, 2], ALU.add)

        def norm(dve, ch, xin, lo, w, groups, mean_over, var_over, centre, s_centred, s_squared, dst, relu):
            cols = slice(lo, lo + w)
            if centre:
                ch.step(nc.vector.tensor_reduce(st[:, 0, :], xin[:, :, cols], AX.X, ALU.add))
                ch.step(nc.vector.tensor_scalar(st[:, 1, :], st[:, 0, :], 1.0 / mean_over, None, ALU.mult))
                ch.step(nc.vector.tensor_tensor(dst[:, :, cols], xin[:, :, cols],
                                                ax(st[:, 1, :], (1, NT), (0, w)), ALU.subtract))
                base = dst
            else:
                base = xin
            ch.step(nc.vector.tensor_tensor(TAB[:, :, cols], base[:, :, cols], base[:, :, cols], ALU.mult))
            ch.step(nc.vector.tensor_reduce(st[:, 2, :], TAB[:, :, cols], AX.X, ALU.add))
            ch.step(nc.vector.tensor_scalar(st[:, 3, :], st[:, 2, :], 1.0 / var_over, EPS, ALU.mult, ALU.add))
            nc.vector.tensor_copy(st[:, 4, :], st[:, 3, :]).then_inc(s_centred, 1)
            dve.wait_ge(s_squared, 1)
            ch.step(nc.vector.reciprocal(st[:, 5, :], st[:, 0, :]))
            ch.step(nc.vector.tensor_tensor(dst[:, :, cols], base[:, :, cols],
                                            ax(st[:, 5, :], (1, NT), (0, w)), ALU.mult))
            if relu:
                ch.step(nc.vector.tensor_scalar(dst[:, :, cols], dst[:, :, cols], 0.0, None, ALU.max))

        s_nc = [sem(f"s_nc{i}") for i in range(4)]
        s_ns = [sem(f"s_ns{i}") for i in range(4)]

        block = ctx.enter_context(nc.Block())

        n_const = [0]
        @block.sync
        def _(sp):
            n = 0

            def load(dst, src):
                nonlocal n
                sp.dma_start(dst, src).then_inc(s_const, 16)
                n += 1

            def rows(v):
                return v.rearrange("(f a) -> f a", a=1)
            load(X[:, :, :], a["x"].rearrange("(j p) f -> p j f", p=P))
            load(ident[:, :], a["c_ident"])
            load(iota[:, :], a["c_iota"])
            load(nodecon[:, :, :], a["c_nodecon"])
            load(vcol[:, :], a["c_vcol"])
            load(tplus[:, :], a["c_tplus"])
            load(last[:, :], a["last"])
            load(dstw, bass.AP(a["drow"].tensor, 0, [[EP // P, P], [1, EP // P + 1]]))
            load(attr[:, :], a["attr"])
            load(w_ms0[:, 0:64], a["W_alpha"])
            load(w_ms0[:, 96:160], a["Ws_val"])
            load(w_mv0[:, :], a["Wv_val"])
            load(w_hs0[:, :], a["Ws_vlin"])
            load(w_hv0[:, :], a["Wv_vlin"])
            load(w2s[0:64, :], rows(a["w2_ss"]))
            load(w2s[64:96, :], rows(a["w2_vv0"]))
            load(w2v[0:64, :], rows(a["w2_sv"]))
            load(w2v[64:96, :], rows(a["w2_vs"]))
            load(w2v[96:128, :], rows(a["w2_vv1"]))
            load(ws_val_t[:, :], a["Ws_val_T"])
            load(wg[:, :], a["Wg"])
            load(adot[:, :], a["adot_rep"])
            load(gam_s[:, :], rows(a["gamma_s"]))
            load(bet_s[:, :], rows(a["beta_s"]))
            load(n0s[:, 0:S], a["Ws_src"])
            load(n0s[:, S:2 * S], a["Ws_dst"])
            load(e0s[:, :], a["Wps"])
            load(n1s[:, 0:96], a["sc_ws"])
            load(n1s[:, 96:160], a["lin1_ws"])
            load(fc1[:, 0:64], a["fc_w1"])
            load(fc1[:, 64:128], a["fc_w1"])
            load(l2s[:, :], a["lin2_ws"])
            load(l2v[:, :], a["lin2_wv"])
            sp.wait_ge(s_zero, 6)
            load(w_edge1[0:64, 0:64], a["fc_w2"][:, 0:64])
            load(w_edge1[0:64, 64:96], a["fc_w2"][:, 128:160])
            for k in range(3):
                rs, b = slice(64 * ((k + 1) % 2), 64 * ((k + 1) % 2) + 64), 96 + P * k
                load(w_edge1[rs, b:b + 64], a["fc_w2"][:, 64:128])
                load(w_edge1[rs, b + 64:b + 128], a["fc_w2"][:, 160:224])
            for k in range(3):
                r, c = slice(C * k, C * k + C), C * k
                load(gam_v[r, :], rows(a["gamma_v"]))
                load(n0v[r, c:c + C], a["Wv_src"])
                load(n0v[r, 96 + c:96 + c + C], a["Wv_dst"])
                load(e0v[r, c:c + C], a["Wpv"])
                load(n1v[r, c:c + C], a["sc_wv"])
                load(n1v[r, 96 + c:96 + c + C], a["lin1_wv"])
                rr, b = slice(16 * (k + 1), 16 * (k + 2)), 96 + P * k
                load(w_edge0[rr, b:b + 64], a["W_rbf"][:, 64:128])
                load(w_edge0[rr, b + 64:b + 128], a["W_rbf"][:, 160:224])
            load(w_edge0[0:16, 0:64], a["W_rbf"][:, 0:64])
            load(w_edge0[0:16, 64:96], a["W_rbf"][:, 128:160])
            n_const[0] = n

            sp.wait_ge(s_tcol, 1)
            with nc.allow_non_contiguous_dma(reason="512 words once"):
                for r in range(2):
                    sp.dma_start(vis_tab.ap()[r, :].rearrange("(c p) -> p c", p=P), tcoli[:, r, :]).then_inc(s_vst, 16)
            sp.wait_ge(s_vst, 32)
            sp.dma_start(vis[:, :, :].rearrange("a r v -> a (r v)"),
                         vis_tab.ap().rearrange("(a r) v -> a (r v)", a=1)).then_inc(s_vis, 16)
            sp.wait_ge(s_vis, 16)
            sp.wait_ge(s_tab0, 1)
            sp.dma_start(src_tab.ap().rearrange("(j p) f -> p j f", p=P), TAB[:, :, :]).then_inc(s_tab0d, 16)

            def visit_loads(v, total, L, free, extra):
                if not inside(v, total):
                    return
                T = v.chunk(sp)
                if v.reused():
                    sp.wait_ge(L[free], v.num - (U - 1))
                s = v.slot
                sp.dma_start(sd[:, s, :], a["sd"][bass.ds(T, 1)].rearrange("t p c -> (t p) c")).then_inc(L["ld"][s], 16)
                sp.dma_start(yed[:, s, :], a["yed"][bass.ds(T, 1)].rearrange("t p c -> (t p) c")).then_inc(L["ld"][s], 16)
                extra(T, s)

            def extra0(T, s):
                row = a["drow"][bass.ds(T, 1), :]
                sp.dma_start(drow[:, s, :], row.to_broadcast([P, CH])).then_inc(LA["ld"][s], 16)
                for k in range(4):
                    yr = a["yT"][k:k + 1, bass.ds(T, 1), :].rearrange("a t e -> a (t e)")
                    sp.dma_start(yrep[16 * k:16 * k + 16, s, 0, :], yr.to_broadcast([16, CH])).then_inc(LA["ld"][s], 16)
                rb = a["rbfT"][:, bass.ds(T, 1), :].rearrange("r t e -> r (t e)")
                for k in range(4):
                    sp.dma_start(rrep[16 * k:16 * k + 16, s, :], rb).then_inc(LA["ld"][s], 16)

            def extra1(T, s):
                for k in range(4):
                    yr = a["yT"][k:k + 1, bass.ds(T, 1), :].rearrange("a t e -> a (t e)")
                    sp.dma_start(yrep[64 * (k % 2):64 * (k % 2) + 64, s, k // 2, :],
                                 yr.to_broadcast([64, CH])).then_inc(LB["ld"][s], 16)
                sp.dma_start(rrep[:, s, :], a["e64T"][:, bass.ds(T, 1), :].rearrange("r t e -> r (t e)"))\
                    .then_inc(LB["ld"][s], 16)

            loop_visits(sp, 0, 0, lambda v, total: visit_loads(v, total, LA, "m2", extra0))

            sp.wait_ge(s_tab1, 1)
            sp.dma_start(hid_tab.ap().rearrange("(j p) f -> p j f", p=P), TAB[:, :, :]).then_inc(s_tab1d, 16)
            loop_visits(sp, 0, 0, lambda v, total: visit_loads(v, total, LB, "sc", extra1))

            sp.wait_ge(s_out, 1)
            sp.dma_start(out.rearrange("(j p) f -> p j f", p=P), X[:, :, :]).then_inc(s_outd, 16)
            sp.wait_ge(s_outd, 16)
            sp.wait_ge(s_tab0d, 16)
            sp.wait_ge(s_tab1d, 16)

        n_loads = n_const[0]

        @block.gpsimd
        def _(pool):
            ch = Chain(pool, s_pool)
            nc.gpsimd.memset(ones[:, :], 1.0)
            for t in (gam_v, n0v, e0v, n1v, w_edge0, w_edge1):
                nc.gpsimd.memset(t[:, :], 0.0).then_inc(s_zero, 1)
            nc.gpsimd.memset(m_run[:, :, :], NEG)
            nc.gpsimd.memset(ACC[:, :, :], 0.0).then_inc(s_prep, 1)
            pool.wait_ge(s_vis, 16)
            pool.wait_ge(s_tab0d, 16)

            def wait(sem, count):
                pool.wait_ge(sem, count)
                pool.sem_inc(s_passed, 1)

            def gathers(v, L, tab, nld):
                s = v.slot
                wait(L["ld"][s], v.round(16 * nld))
                for g in range(G):
                    pool.indirect_dma_start(gat[:, s, g * D:(g + 1) * D], None, tab.ap(),
                                            bass.IndirectOffsetOnAxis(ap=sd[:, s, g:g + 1], axis=0))\
                        .then_inc(L["ga"][s], 16)

            def columns(v, L):
                s = v.slot
                J = v.node_tile(pool)
                nc.gpsimd.tensor_copy(ncol[:, s, :], nodecon[:, bass.ds(J, 1), :].rearrange("p a f -> p (a f)"))
                nc.gpsimd.tensor_copy(sdf[:, s, :], sd[:, s, G:2 * G]).then_inc(L["cvt"], 1)
                wait(L["cvt"], v.num + 1)

            def one_hot_edges(v):
                s = v.slot
                for g in range(G):
                    ins = nc.gpsimd.tensor_scalar(ohE[:, s, g, :], iota[:, :], sdf[:, s, g:g + 1],
                                                  ncol[:, s, 1:2], ALU.subtract, ALU.is_equal)
                return ins

            def stage0(v, total):
                if not inside(v, total):
                    return
                s = v.slot
                gathers(v, LA, src_tab, 11)
                nc.gpsimd.tensor_tensor(zt[:, s, :], rrep[:, s, :], yrep[0:64, s, 0, :], ALU.mult).then_inc(LA["z"], 1)
                if v.reused():
                    wait(LA["sc"], v.num - (U - 1))
                columns(v, LA)
                nc.gpsimd.tensor_scalar(ohT[:, s, :], drow[:, s, :], ncol[:, s, 0:1], None, ALU.is_equal)\
                    .then_inc(LA["oht"], 1)
                wait(LA["oht"], v.num + 1)
                nc.gpsimd.tensor_scalar(mneg[:, s, :], ohT[:, s, :], 1.0, -NEG, ALU.subtract, ALU.mult)
                one_hot_edges(v).then_inc(LA["oh"], 1)
            loop_visits(pool, 0, 0, stage0)
            pool.wait_ge(s_nrm[0], 1)
            nc.gpsimd.memset(ACC[:, :, :], 0.0).then_inc(s_prep, 1)
            pool.wait_ge(s_tab1d, 16)

            def stage1(v, total):
                if not inside(v, total):
                    return
                gathers(v, LB, hid_tab, 7)
                if v.reused():
                    wait(LB["sc"], v.num - (U - 1))
                columns(v, LB)
                one_hot_edges(v).then_inc(LB["oh"], 1)
            loop_visits(pool, 0, 0, stage1)

        @block.tensor
        def _(pe):
            pe.wait_ge(s_const, 16 * n_loads)
            nc.tensor.matmul(DM[0:96, 0:C], ws_val_t[:, :], wg[:, :], start=True, stop=True).then_inc(s_wsg, 1)
            pe.wait_ge(s_bnd, 2)
            pe.wait_ge(s_prep, 1)
            nc.tensor.matmul(AG[0:1, 0:1], down[:, EP // P:EP // P + 1], onec[:, :], start=True, stop=True)\
                .then_inc(s_wsg, 1)
            nc.tensor.matmul(E1[:, :, :].rearrange("p g f -> p (g f)")[:, 0:NCH], ones[:, :], lastf[:, :],
                             start=True, stop=True).then_inc(s_wsg, 1)

            pe.wait_ge(s_nrm[1], 1)
            node_pe(pe, "n0", [(S, 96), (0, S)], [
                (ax(DM[:, 0:1], (D, 2), (1, S)), tr_n[0:S, 1, :], n0s[:, :].rearrange("p (a f) -> p a f", a=2)),
                (ax(DM[:, S:S + 1], (D, 2), (1, 96)), tr_n[0:96, 0, :], n0v[:, :].rearrange("p (a f) -> p a f", a=2))])

            def pre0(v, total):
                if not inside(v, total):
                    return
                s = v.slot
                J = v.node_tile(pe)
                pe.wait_ge(LA["z"], v.num + 1)
                pe.wait_ge(LA["oh"], v.num + 1)
                if v.base is not None or v.first >= 1:
                    pe.wait_ge(LA["m"], v.num)
                for g in range(G):
                    es = slice(g * P, g * P + P)
                    nc.tensor.matmul(W[:, g, 0:MW], zt[:, s, es], w_edge0[:, :], start=True, stop=True)
                    ins = nc.tensor.matmul(DM[:, g * D:(g + 1) * D], ohT[:, s, es],
                                           DT[:, bass.ds(J, 1), :].rearrange("p a f -> p (a f)"),
                                           start=True, stop=True)
                ins.then_inc(LA["pre"], 1)

            def turn(Mt, sem_done):
                for b, (lo, w) in enumerate([(0, 96)] + [(96 + P * k, P) for k in range(3)]):
                    for g in range(G):
                        ins = nc.tensor.transpose(TR[0:w, b * G + g, :], Mt[:, g, lo:lo + w], ident[:, :])
                ins.then_inc(sem_done, 1)

            def f2(v, total):
                if not inside(v, total):
                    return
                pe.wait_ge(LA["m"], v.num + 1)
                if v.base is not None or v.first >= 2:
                    pe.wait_ge(LA["c2"], v.num - 1)
                turn(M[:, 0], LA["t1"])
                pe.wait_ge(LA["c1"], v.num + 1)
                if v.base is not None or v.first >= 1:
                    pe.wait_ge(LA["a4"], v.num)
                    pe.wait_ge(LA["sv2"], v.num)
                for g in range(G):
                    nc.tensor.matmul(E1[:, g, 0:160], MT[0:96, 0, g, :], w_ms0[:, :], start=True, stop=True)
                    for k in range(3):
                        ins = nc.tensor.matmul(E1[:, g, 160 + C * k:160 + C * (k + 1)], MT[:, 1 + k, g, :], w_mv0[:, :],
                                               start=True, stop=True)
                ins.then_inc(LA["e1"], 1)

            def ab(v, total):
                if not inside(v, total):
                    return
                pe.wait_ge(LA["a4"], v.num + 1)
                if total is None or v.first + 1 < total:
                    pe.wait_ge(LA["c1"], v.num + 2)
                for h in range(H):
                    for g in range(G):
                        ins = nc.tensor.transpose(TR[:, h * G + g, :], ax(a4[:, v.slot, g, h:h + 1], (0, P)), ident[:, :])
                ins.then_inc(LA["ab"], 1)

            def t2(v, total):
                if not inside(v, total):
                    return
                pe.wait_ge(LA["m2"], v.num + 1)
                pe.wait_ge(LA["mx"], v.num + 1)
                turn(M2, LA["t2"])
                pe.wait_ge(LA["c2"], v.num + 1)
                if v.base is not None or v.first >= 1:
                    pe.wait_ge(LA["hx"], v.num)
                for g in range(G):
                    hp = HP[:, g * D:(g + 1) * D].rearrange("p (h f) -> p h f", h=H)
                    nc.tensor.matmul(hp[:, :, 0:16], MT2[0:96, 0, g, :], w_hs0[:, :].rearrange("p (h f) -> p h f", h=H),
                                     start=True, stop=True)
                    for k in range(3):
                        nc.tensor.matmul(hp[:, :, 16 + 8 * k:24 + 8 * k], MT2[:, 1 + k, g, :],
                                         w_hv0[:, :].rearrange("p (h f) -> p h f", h=H), start=True, stop=True)
                    ins = nc.tensor.matmul(HP[:, G * D + g * H:G * D + (g + 1) * H], ohT[:, v.slot, g * P:(g + 1) * P],
                                           mn[:, v.slot, :], start=True, stop=True)
                ins.then_inc(LA["h"], 1)

            def sc0(v, total):
                if not inside(v, total):
                    return
                pe.wait_ge(LA["hx"], v.num + 1)
                pe.wait_ge(LA["exs"], v.num + 1)
                if v.base is not None or v.first >= 1:
                    pe.wait_ge(LA["acc"], v.num)
                for g in range(G):
                    ins = nc.tensor.matmul(AG[:, 0:H * HW], ohE[:, v.slot, g, :],
                                           HX[:, g].rearrange("p h f -> p (h f)"), start=(g == 0), stop=(g == G - 1))
                ins.then_inc(LA["sc"], 1)

            def stage0(t, total):
                t2(t + -2, total)
                f2(t, total)
                sc0(t + -2, total)
                pre0(t + 1, total)
                ab(t + -1, total)
            pe.wait_ge(s_prep, 3)
            pe.wait_ge(s_tab0, 1)
            pe.wait_ge(s_vis, 16)
            loop_visits(pe, 1, 2, stage0)

            pe.wait_ge(s_nrm[0], 1)
            node_pe(pe, "e0", [(S, 96), (0, S)], [
                (DM[:, 0:S], tr_n[0:S, 1, :], e0s[:, :]), (DM[:, S:D], tr_n[0:96, 0, :], e0v[:, :])])
            pe.wait_ge(s_nrm[2], 1)
            node_pe(pe, "n1", [(S, 96), (0, S)], [
                (DM[:, 0:160], tr_n[0:S, 1, :], n1s[:, :]), (DM[:, 160:352], tr_n[0:96, 0, :], n1v[:, :])])

            def fc(v, total):
                if not inside(v, total):
                    return
                pe.wait_ge(LB["ld"][v.slot], v.round(16 * 7))
                if v.base is not None or v.first >= 1:
                    pe.wait_ge(LB["hid"], v.num)
                nc.tensor.matmul(DM[:, 0:CH], fc1[:, :], rrep[:, v.slot, :], start=True, stop=True).then_inc(LB["fc"], 1)

            def w1(v, total):
                if not inside(v, total):
                    return
                pe.wait_ge(LB["hy"], v.num + 1)
                if v.base is not None or v.first >= 2:
                    pe.wait_ge(LB["m"], v.num - 1)
                for g in range(G):
                    for kk, (lo, w) in enumerate(((0, 96 + P), (96 + P, 2 * P))):
                        ins = nc.tensor.matmul(Wr[v.par][:, g, lo:lo + w], hidy[:, v.par, kk, g * P:(g + 1) * P],
                                               w_edge1[:, lo:lo + w], start=True, stop=True)
                ins.then_inc(LB["w"], 1)

            def sc1(v, total):
                if not inside(v, total):
                    return
                pe.wait_ge(LB["oh"], v.num + 1)
                pe.wait_ge(LB["m"], v.num + 1)
                if v.base is not None or v.first >= 1:
                    pe.wait_ge(LB["acc"], v.num)
                for g in range(G):
                    ins = nc.tensor.matmul(AG[:, 0:MW], ohE[:, v.slot, g, :], M[:, v.par, g, :],
                                           start=(g == 0), stop=(g == G - 1))
                ins.then_inc(LB["sc"], 1)

            def stage1(t, total):
                w1(t + 1, total)
                fc(t + 3, total)
                sc1(t, total)
            pe.wait_ge(s_tab1, 1)
            loop_visits(pe, 3, 0, stage1)
            pe.wait_ge(s_nrm[3], 1)
            node_pe(pe, "fi", [(0, 96)] + [(96 + P * k, P) for k in range(3)], [
                (DM[:, 0:96], tr_n[0:96, 0, :], l2s[:, :])] + [
                (DM[:, 96 + C * k:96 + C * (k + 1)], tr_n[:, 1 + k, :], l2v[:, :]) for k in range(3)])

        @block.scalar
        def _(act):
            def root(i):
                act.wait_ge(s_nc[i], 1)
                nc.scalar.activation(st[:, 0, :], st[:, 4, :], ACT.Sqrt).then_inc(s_ns[i], 1)
            for i in range(3):
                root(i)
            act.wait_ge(s_nrm[1], 1)
            node_act(act, "n0", XN, D)

            def dup(v, total, L, wait_name, src, sem_done):
                if not inside(v, total):
                    return
                act.wait_ge(L[wait_name], v.num + 1)
                nc.scalar.activation(src[:, :, D:D + 64], src[:, :, S:S + 64], ACT.Copy).then_inc(L[sem_done], 1)

            def copies(v, total, turned, dst, sem_done, freed):
                if not inside(v, total):
                    return
                act.wait_ge(LA[turned], v.num + 1)
                if v.base is not None or v.first >= 1:
                    act.wait_ge(LA[freed], v.num)
                nc.scalar.activation(dst[0:96, 0].rearrange("p g e -> p (g e)"),
                                     TR[0:96, 0:G, :].rearrange("p g e -> p (g e)"), ACT.Copy)
                nc.scalar.activation(dst[:, 1:4].rearrange("p k g e -> p (k g e)"),
                                     TR[:, G:4 * G, :].rearrange("p a e -> p (a e)"), ACT.Copy).then_inc(LA[sem_done], 1)

            def tanh(v, total):
                if not inside(v, total):
                    return
                act.wait_ge(LA["e1"], v.num + 1)
                if v.base is not None or v.first >= 2:
                    act.wait_ge(LA["sv2"], v.num - 1)
                nc.scalar.activation(th[:, v.par], E1[:, :, 64:160], ACT.Tanh, scale=0.5).then_inc(LA["th"], 1)

            def exps(v, total):
                if not inside(v, total):
                    return
                act.wait_ge(LA["d"], v.num + 1)
                if v.base is not None or v.first >= 1:
                    act.wait_ge(LA["hx"], v.num)
                    act.wait_ge(LA["sc"], v.num)
                nc.scalar.activation(cor[:, v.slot, :], mdf[:, v.slot, :], ACT.Exp)
                nc.scalar.activation(ex[:, :], ad[:, :], ACT.Exp).then_inc(LA["ex"], 1)
                act.wait_ge(LA["ex"], v.num + 1)
                nc.scalar.activation(HX[:, :, :, HW - 1].rearrange("p g h -> p (g h)") if False else
                                     ax(HX[:, 0, 0, HW - 1:HW], (HW, G * H)), ex[:, :], ACT.Copy)\
                    .then_inc(LA["exs"], 1)

            def stage0(t, total):
                dup(t, total, LA, "msg", SV, "dup")
                copies(t + -2, total, "t2", MT2, "c2", "h")
                exps(t + -2, total)
                copies(t, total, "t1", MT, "c1", "e1")
                tanh(t, total)
                dup(t + -1, total, LA, "sv2", SV2, "dup2")
            loop_visits(act, 0, 2, stage0)
            act.wait_ge(s_nrm[0], 1)
            node_act(act, "e0", XN, D)
            root(3)
            act.wait_ge(s_nrm[2], 1)
            node_act(act, "n1", HN, D)

            def stage1(t, total):
                v = t + 3
                if inside(v, total):
                    act.wait_ge(LB["fc"], v.num + 1)
                    if v.base is not None or v.first >= 2:
                        act.wait_ge(LB["hy"], v.num - 1)
                    nc.scalar.activation(hid[:, v.par, :], DM[:, 0:CH], ACT.Silu, scale=0.125).then_inc(LB["hid"], 1)
                v = t
                if inside(v, total):
                    act.wait_ge(LB["ga"][v.slot], v.round(16 * G))
                    if v.base is not None or v.first >= 1:
                        act.wait_ge(LB["m"], v.num)
                    gv = gat[:, v.slot, :].rearrange("p (g f) -> p g f", g=G)
                    nc.scalar.activation(SV[:, :, 0:D], gv, ACT.Copy)
                    nc.scalar.activation(SV[:, :, D:D + 64], gv[:, :, S:S + 64], ACT.Copy).then_inc(LB["dup"], 1)
            loop_visits(act, 3, 0, stage1)
            act.wait_ge(s_nrm[3], 1)
            node_act(act, "fi", ACC, MW)

            act.wait_ge(s_nrm[4], 1)
            nc.scalar.activation(TAB[:, :, 0:64], SC[:, :, 0:64], ACT.Silu)
            nc.scalar.activation(TAB[:, :, 64:96], SC[:, :, 64:96], ACT.Sigmoid).then_inc(s_sq, 1)

        @block.vector
        def _(dve):
            ch = Chain(dve, s_dve)
            TT, TS = nc.vector.tensor_tensor, nc.vector.tensor_scalar
            dve.wait_ge(s_const, 16 * n_loads)
            for w, cols, f in ((w_edge0, 64, R3), (w_edge0, 96, R2)):
                v = ax(w[:, 96 + cols:97 + cols], (P, 3), (1, C))
                TS(v, v, f, None, ALU.mult)
            ws = 1.0 / (8.0 * 4.0)
            for lo, dims, f in ((0, [(1, 96)], ws), (96, [(P, 3), (1, 64)], ws), (160, [(P, 3), (1, C)], ws * R3),
                                (192, [(P, 3), (1, C)], ws * R2)):
                v = ax(w_edge1[:, lo:lo + 1], *dims)
                TS(v, v, f, None, ALU.mult)
            TS(w2s[64:96, :], w2s[64:96, :], R3, None, ALU.mult)
            ch.step(TS(w2v[96:128, :], w2v[96:128, :], R2, None, ALU.mult))
            TS(w_hs0[:, :], w_hs0[:, :], w2s[:, 0:1], None, ALU.mult)
            TS(w_hv0[:, :], w_hv0[:, :], w2v[:, 0:1], None, ALU.mult)
            dve.wait_ge(s_wsg, 1)
            nc.vector.tensor_copy(w_ms0[:, 64:96], DM[0:96, 0:C])
            w = EP // P
            ch.step(TT(down[:, 0:w], dstw[:, 0:w], dstw[:, 1:w + 1], ALU.is_gt))
            ch.step(nc.vector.tensor_reduce(down[:, w:w + 1], down[:, 0:w], AX.X, ALU.max))
            nc.vector.memset(onec[:, :], 1.0).then_inc(s_bnd, 1)
            ch.step(nc.vector.tensor_single_scalar(last[:, :], last[:, :], 7, ALU.arith_shift_right))
            ch.step(nc.vector.tensor_copy(lastf[:, :], last[:, :]))
            TT(lastf[:, :], lastf[:, :], tplus[:, :], ALU.add).then_inc(s_bnd, 1)
            dve.wait_ge(s_wsg, 3)
            ch.step(nc.vector.tensor_copy(flag[:, :], AG[0:1, 0:1]))
            ch.step(nc.vector.tensor_copy(bound[:, :], E1[:, :, :].rearrange("p g f -> p (g f)")[:, 0:NCH]))
            for c in range(U):
                ch.step(TS(cmpv[:, :], bound[:, :], vcol[:, c:c + 1], None, ALU.is_le))
                ch.step(nc.vector.tensor_reduce(tcol[:, 0, c:c + 1], cmpv[:, :], AX.X, ALU.add))
            ch.step(TT(tcol[:, 1, :], vcol[:, :], tcol[:, 0, :], ALU.subtract))
            nc.vector.tensor_copy(tcoli[:, :, :], tcol[:, :, :]).then_inc(s_tcol, 1)

            norm(dve, ch, X, 0, D, 1, D, D, True, s_nc[0], s_ns[0], HN, True)
            norm(dve, ch, HN, 0, S, 1, S, S, True, s_nc[1], s_ns[1], XN, False)
            norm(dve, ch, HN, S, 96, 1, C, C, False, s_nc[2], s_ns[2], XN, False)
            dve.sem_inc(s_nrm[1], 1)

            def node_dve(ph, evac, out_done, copy_out):
                s = nd[ph]

                def body(j, first):
                    dve.wait_ge(s["tr"], j + 1)
                    copy_out().then_inc(s["cp"], 1)
                    dve.wait_ge(s["mm"], j + 1)
                    evac(j).then_inc(s["ev"], 1)
                node_tiles(dve, body)

            def scaled_copy():
                TS(tr_n[0:S, 1, :], TR[0:S, 1, :], gam_s[:, 0:1], bet_s[:, 0:1], ALU.mult, ALU.add)
                return TS(tr_n[0:96, 0, :], TR[0:96, 0, :], gam_v[:, 0:1], None, ALU.mult)

            def plain_copy():
                nc.vector.tensor_copy(tr_n[0:S, 1, :], TR[0:S, 1, :])
                return nc.vector.tensor_copy(tr_n[0:96, 0, :], TR[0:96, 0, :])

            def tile_of(t, j):
                return t[:, bass.ds(j, 1)].rearrange("p a f -> p (a f)")

            def evac_n0(j):
                nc.vector.tensor_copy(tile_of(TAB, j), DM[:, 0:D])
                return nc.vector.tensor_copy(tile_of(DT, j), DM[:, D:2 * D])
            dve.wait_ge(s_prep, 1)
            node_dve("n0", evac_n0, None, scaled_copy)
            dve.wait_ge(nd["n0"]["ev"], NT)
            dve.sem_inc(s_tab0, 1)
            dve.sem_inc(s_prep, 2)
            ch.wait()
            dve.wait_ge(s_vis, 16)

            def a_part(v, total):
                if not inside(v, total):
                    return
                s = v.slot
                dve.wait_ge(LA["ga"][s], v.round(16 * G))
                dve.wait_ge(LA["pre"], v.num + 1)
                gv = gat[:, s, :].rearrange("p (g f) -> p g f", g=G)
                TT(SV[:, :, 0:D], gv, DM[:, 0:G * D].rearrange("p (g f) -> p g f", g=G), ALU.add)\
                    .then_inc(LA["msg"], 1)
                dve.wait_ge(LA["msg"], v.num + 1)
                if v.base is not None or v.first >= 1:
                    dve.wait_ge(LA["t1"], v.num)
                products(dve, ch, SV, W[:, :, 0:S],
                         lambda g: ax(W[:, g, 96:97], (P, 3), (1, S)),
                         lambda g: ax(W[:, g, 64:65], (0, 3), (1, C)),
                         lambda g: ax(W[:, g, 160:161], (P, 3), (1, C)),
                         lambda g: ax(W[:, g, 192:193], (P, 3), (1, C)),
                         M[:, 0], lambda: dve.wait_ge(LA["dup"], v.num + 1)).then_inc(LA["m"], 1)

            def hx_part(v, total):
                if not inside(v, total):
                    return
                s = v.slot
                dve.wait_ge(LA["h"], v.num + 1)
                ch.step(TT(ad[:, :], a4[:, s].rearrange("p g h -> p (g h)"), HP[:, G * D:G * D + G * H], ALU.subtract))
                TS(ad[:, :], ad[:, :], 0.0, None, ALU.min).then_inc(LA["d"], 1)
                dve.wait_ge(LA["ex"], v.num + 1)
                if v.base is not None or v.first >= 1:
                    dve.wait_ge(LA["sc"], v.num)
                TT(ax(HX[:, 0, 0, 0:1], (HW, G * H), (1, D // H)), ax(HP[:, 0:1], (D // H, G * H), (1, D // H)),
                   ax(ex[:, 0:1], (1, G * H), (0, D // H)), ALU.mult).then_inc(LA["hx"], 1)

            def b1_part(v, total):
                if not inside(v, total):
                    return
                s = v.slot
                dve.wait_ge(LA["th"], v.num + 1)
                ch.add(TS(sig[:, :, :], th[:, v.par], 0.5, 0.5, ALU.mult, ALU.add))
                ch.step(nc.vector.scalar_tensor_tensor(lk[:, :, :], E1[:, :, 0:S], 0.2, E1[:, :, 0:S], ALU.mult, ALU.max)
                        if False else TS(lk[:, :, :], E1[:, :, 0:S], 0.2, None, ALU.mult))
                ch.add(TT(lk2[:, :, :], E1[:, :, 0:S], lk[:, :, :], ALU.max))
                for g in range(G):
                    TT(SV2[:, g, S:D].rearrange("p (k c) -> p k c", k=3),
                       E1[:, g, 160:256].rearrange("p (k c) -> p k c", k=3), ax(sig[:, g, 0:1], (0, 3), (1, C)), ALU.mult)
                nc.vector.tensor_copy(SV2[:, :, 0:S], sig[:, :, C:96]).then_inc(LA["sv2"], 1)
                ch.wait()
                ch.step(TT(lk[:, :, :], lk2[:, :, :], ax(adot[:, 0:1], (0, G), (1, S)), ALU.mult))
                nc.vector.tensor_reduce(a4[:, s].rearrange("p g h -> p (g h)"),
                                        ax(lk[:, 0, 0:1], (16, G * H), (1, 16)), AX.X, ALU.add).then_inc(LA["a4"], 1)

            def acc_part(v, total):
                if not inside(v, total):
                    return
                J = v.node_tile(dve)
                tj = accA[:, bass.ds(J, 1), :].rearrange("p a f -> p (a f)")
                if v.base is not None or v.first >= 1:
                    dve.wait_ge(LA["acc"], v.num)
                ch.step(TT(atmp[:, :, :], tj.rearrange("p (h f) -> p h f", h=H),
                           ax(cor[:, v.slot, 0:1], (1, H), (0, HW)), ALU.mult))
                dve.wait_ge(LA["sc"], v.num + 1)
                TT(tj, atmp[:, :, :].rearrange("p h f -> p (h f)"), AG[:, 0:H * HW], ALU.add).then_inc(LA["acc"], 1)

            def m2_part(v, total):
                if not inside(v, total):
                    return
                y = yed[:, v.slot, :].rearrange("p (g k) -> p g k", g=G)
                dve.wait_ge(LA["sv2"], v.num + 1)
                if v.base is not None or v.first >= 1:
                    dve.wait_ge(LA["t2"], v.num)
                products(dve, ch, SV2, ax(y[:, 0, 0:1], (4, G), (0, S)),
                         lambda g: ax(y[:, g, 1:2], (1, 3), (0, S)),
                         lambda g: ax(y[:, g, 0:1], (0, 3), (0, C)),
                         lambda g: ax(y[:, g, 1:2], (1, 3), (0, C)),
                         lambda g: ax(y[:, g, 1:2], (1, 3), (0, C)),
                         M2, lambda: dve.wait_ge(LA["dup2"], v.num + 1)).then_inc(LA["m2"], 1)

            def mx_part(v, total):
                if not inside(v, total):
                    return
                s = v.slot
                J = v.node_tile(dve)
                mj = m_run[:, bass.ds(J, 1), :].rearrange("p a f -> p (a f)")
                ch.step(nc.vector.tensor_copy(mo[:, s, :], mj))
                dve.wait_ge(LA["ab"], v.num + 1)
                for h in range(H):
                    ch.step(nc.vector.tensor_tensor_reduce(
                        out=scr[:, :], in0=TR[:, h * G:(h + 1) * G, :].rearrange("p g e -> p (g e)"), in1=mneg[:, s, :],
                        scale=1.0, scalar=mo[:, s, h:h + 1], op0=ALU.add, op1=ALU.max, accum_out=mn[:, s, h:h + 1]))
                nc.vector.tensor_copy(mj, mn[:, s, :])
                TT(mdf[:, s, :], mo[:, s, :], mn[:, s, :], ALU.subtract).then_inc(LA["mx"], 1)

            def stage0(t, total):
                ch.restart()
                a_part(t, total)
                hx_part(t + -2, total)
                b1_part(t + -1, total)
                acc_part(t + -2, total)
                m2_part(t + -1, total)
                mx_part(t + -1, total)
            loop_visits(dve, 0, 2, stage0, lambda total: dve.wait_ge(LA["acc"], total))

            ch.restart()
            aj = accA.rearrange("p j (h f) -> p j h f", h=H)
            den = XN[:, :, 0:H]
            rec = TAB[:, :, 0:H]
            dve.wait_ge(s_tab0d, 16)
            ch.step(TS(den, aj[:, :, :, HW - 1], 1e-16, None, ALU.add))
            ch.step(nc.vector.reciprocal(rec, den))
            for h in range(H):
                r = ax(TAB[:, 0, h:h + 1], (D, NT), (0, 16))
                TT(XN[:, :, 16 * h:16 * h + 16], aj[:, :, h, 0:16], r, ALU.mult)
                for k in range(3):
                    r = ax(TAB[:, 0, h:h + 1], (D, NT), (0, 8))
                    lo = S + C * k + 8 * h
                    ins = TT(XN[:, :, lo:lo + 8], aj[:, :, h, 16 + 8 * k:24 + 8 * k], r, ALU.mult)
            ch.step(ins)
            dve.sem_inc(s_nrm[0], 1)
            ch.step(TT(X[:, :, :], X[:, :, :], HN[:, :, :], ALU.add))

            def evac_e0(j):
                return TT(tile_of(X, j), tile_of(X, j), DM[:, 0:D], ALU.add)
            node_dve("e0", evac_e0, None, plain_copy)
            dve.wait_ge(nd["e0"]["ev"], NT)
            norm(dve, ch, X, 0, D, 1, D, D, True, s_nc[3], s_ns[3], HN, True)
            dve.sem_inc(s_nrm[2], 1)

            def evac_n1(j):
                nc.vector.tensor_copy(tile_of(SC, j)[:, 0:96], DM[:, 0:96])
                nc.vector.tensor_copy(tile_of(SC, j)[:, 96:192], DM[:, 160:256])
                nc.vector.tensor_copy(tile_of(TAB, j)[:, 0:S], DM[:, 96:160])
                return nc.vector.tensor_copy(tile_of(TAB, j)[:, S:D], DM[:, 256:352])
            node_dve("n1", evac_n1, None, plain_copy)
            dve.wait_ge(nd["n1"]["ev"], NT)
            cs, cv = S ** -0.5, C ** -0.5
            ch.step(TT(TAB[:, :, :], TAB[:, :, :], ax(attr[:, 0:1], (1, NT), (0, D)), ALU.mult))
            TS(TAB[:, :, 0:S], TAB[:, :, 0:S], cs, None, ALU.mult)
            ch.step(TS(TAB[:, :, S:D], TAB[:, :, S:D], cv, None, ALU.mult))
            dve.sem_inc(s_tab1, 1)
            dve.wait_ge(s_prep, 4)

            def hy(v, total):
                if not inside(v, total):
                    return
                dve.wait_ge(LB["hid"], v.num + 1)
                if v.base is not None or v.first >= 2:
                    dve.wait_ge(LB["w"], v.num - 1)
                for kk in range(2):
                    ins = TT(hidy[:, v.par, kk, :], hid[:, v.par, :], yrep[:, v.slot, kk, :], ALU.mult)
                ins.then_inc(LB["hy"], 1)

            def m_part(v, total):
                if not inside(v, total):
                    return
                dve.wait_ge(LB["dup"], v.num + 1)
                dve.wait_ge(LB["w"], v.num + 1)
                if v.base is not None or v.first >= 2:
                    dve.wait_ge(LB["sc"], v.num - 1)
                w = Wr[v.par]
                products(dve, ch, SV, w[:, :, 0:S],
                         lambda g: ax(w[:, g, 96:97], (P, 3), (1, S)),
                         lambda g: ax(w[:, g, 64:65], (0, 3), (1, C)),
                         lambda g: ax(w[:, g, 160:161], (P, 3), (1, C)),
                         lambda g: ax(w[:, g, 192:193], (P, 3), (1, C)),
                         M[:, v.par], lambda: None).then_inc(LB["m"], 1)

            def acc1(v, total):
                if not inside(v, total):
                    return
                J = v.node_tile(dve)
                dve.wait_ge(LB["sc"], v.num + 1)
                if v.base is not None or v.first >= 1:
                    dve.wait_ge(LB["acc"], v.num)
                TT(tile_of(ACC, J), tile_of(ACC, J), AG[:, 0:MW], ALU.add).then_inc(LB["acc"], 1)

            def stage1(t, total):
                ch.restart()
                m_part(t, total)
                hy(t + 2, total)
                acc1(t + -1, total)
            loop_visits(dve, 2, 1, stage1, lambda total: dve.wait_ge(LB["acc"], total))
            ch.restart()
            TS(SC[:, :, 0:96], SC[:, :, 0:96], cs, None, ALU.mult)
            ch.step(TS(SC[:, :, 96:192], SC[:, :, 96:192], cv, None, ALU.mult))
            dve.sem_inc(s_nrm[3], 1)

            def four_copies():
                nc.vector.tensor_copy(tr_n[0:96, 0, :], TR[0:96, 0, :])
                return nc.vector.tensor_copy(tr_n[:, 1:4, :], TR[:, 1:4, :])

            def evac_fi(j):
                TS(o_n[:, 0:96], DM[:, 0:96], 96.0 ** -0.5, None, ALU.mult)
                ch.add(TS(o_n[:, 96:192], DM[:, 96:192], 128.0 ** -0.5, None, ALU.mult))
                ch.wait()
                ins = TT(tile_of(SC, j), tile_of(SC, j), o_n[:, :], ALU.add)
                return ins
            s = nd["fi"]

            def body(j, first):
                ch.restart()
                dve.wait_ge(s["tr"], j + 1)
                four_copies().then_inc(s["cp"], 1)
                dve.wait_ge(s["mm"], j + 1)
                if not first:
                    dve.wait_ge(s["ev"], j)
                evac_fi(j).then_inc(s["ev"], 1)
            node_tiles(dve, body)
            dve.wait_ge(s["ev"], NT)
            ch.restart()
            ch.step(TT(SC[:, :, :], SC[:, :, :], ax(attr[:, 0:1], (1, NT), (0, 192)), ALU.mult))
            dve.wait_ge(s_tab1d, 16)
            dve.sem_inc(s_nrm[4], 1)
            dve.wait_ge(s_sq, 1)
            for k in range(3):
                ins = TT(SC[:, :, 96 + C * k:96 + C * (k + 1)], SC[:, :, 96 + C * k:96 + C * (k + 1)],
                         TAB[:, :, 64:96], ALU.mult)
            ch.step(ins)
            TT(X[:, :, 0:S], X[:, :, 0:S], TAB[:, :, 0:S], ALU.add)
            ch.step(TT(X[:, :, S:D], X[:, :, S:D], SC[:, :, 96:192], ALU.add))
            dve.sem_inc(s_out, 1)


def _columns():
    return np.concatenate([np.arange(S)] + [S + 3 * np.arange(C) + k for k in range(3)])


def kernel(**inputs):
    import concourse.bacc as bacc
    from concourse.bass_utils import run_bass_kernel_spmd

    g = {k: np.ascontiguousarray(v) for k, v in inputs.items()}
    perm = _columns()

    def chunks(v, pad):
        full = np.full((EP,) + v.shape[1:], pad, v.dtype)
        full[:E] = v
        return full

    src, dst = chunks(g["src"].astype(np.int32), 0), chunks(g["dst"].astype(np.int32), NP - 1)
    y, rbf, e64 = chunks(g["edge_attr_4"], 0), chunks(g["edge_attr_16"], 0), chunks(g["edge_attr_64"], 0)
    x = np.zeros((NP, D), np.float32)
    x[:N] = g["x"][:, perm]
    attr = np.zeros((NP, 1), np.float32)
    attr[:N] = g["node_vec1"]
    tile = lambda v: v.reshape(NCH, G, P, -1).transpose(0, 2, 1, 3)
    arr = {
        "x": x, "attr": attr.reshape(NT, P).T,
        "sd": np.concatenate([tile(src)[..., 0], tile(dst)[..., 0]], -1),
        "drow": np.concatenate([dst, np.full(CH, NP - 1, np.int32)]).reshape(NCH + 1, CH),
        "last": dst.reshape(NCH, CH)[:, CH - 1][None],
        "yed": tile(y).reshape(NCH, P, G * 4),
        "yT": y.T.reshape(4, NCH, CH),
        "rbfT": rbf.T.reshape(16, NCH, CH),
        "e64T": e64.T.reshape(64, NCH, CH),
        "Ws_val_T": g["L0_gnn_Ws_val"].T,
        "adot_rep": np.broadcast_to(g["L0_gnn_alpha_dot"].reshape(1, S), (P, S)),
        "c_ident": np.eye(P, dtype=np.float32),
        "c_iota": np.broadcast_to(np.arange(P, dtype=np.float32), (P, P)),
        "c_nodecon": np.stack([np.arange(P)[:, None] + P * np.arange(NT)[None],
                               np.broadcast_to(-P * np.arange(NT), (P, NT))], -1).astype(np.float32),
        "c_vcol": (np.arange(P)[:, None] + P * np.arange(U)[None]).astype(np.float32),
        "c_tplus": np.arange(1, NCH + 1, dtype=np.float32)[None],
    }
    for k, v in g.items():
        if k.startswith("L0_gnn_") or k.startswith("L1_gnn_"):
            arr[k[7:]] = v
    arr = {k: np.ascontiguousarray(v) for k, v in arr.items()}
    nc = bacc.Bacc("TRN2", target_bir_lowering=False, num_devices=1)
    aps = {k: nc.dram_tensor("in_" + k, v.shape, mybir.dt.from_np(v.dtype), kind="ExternalInput").ap()
           for k, v in arr.items()}
    out = nc.dram_tensor("out_x", (NP, D), F32, kind="ExternalOutput").ap()
    program(nc, aps, out)
    r = run_bass_kernel_spmd(nc, [{"in_" + k: v for k, v in arr.items()}], core_ids=[0])
    res = r.results[0]["out_x"][:N]
    full = np.empty_like(res)
    full[:, perm] = res
    return full
```

```python
from contextlib import ExitStack

import numpy as np
import concourse.bass as bass
from concourse import mybir

F32 = mybir.dt.float32
I32 = mybir.dt.int32
ALU = mybir.AluOpType
ACT = mybir.ActivationFunctionType
AX = mybir.AxisListType

P = 128
N = 3125
NT = -(-N // P)
NP = NT * P
E = 100000
G = 2
CH = G * P
U = 4
NCH = 392
EP = NCH * CH
VS = NCH + NT - 1
S = 64
C = 32
D = S + 3 * C
H = 4
HW = D // H + 1
MW = 96 + 3 * 128
B0 = ((0, 96), (96, P), (96 + P, P))
M0 = 96 + 2 * P
EPS = 1e-5
NEG = -1e30
R2, R3 = 2.0 ** -0.5, 3.0 ** -0.5
assert VS % U == 0 and NCH * CH >= E


def ax(ap, *dims):
    return bass.AP(ap.tensor, ap.offset, [list(ap.ap[0])] + [list(d) for d in dims])


class Chain:

    def __init__(self, eng, sem):
        self.eng, self.sem, self.n = eng, sem, 0

    def add(self, ins):
        self.n += 1
        return ins.then_inc(self.sem, 1)

    def wait(self):
        self.eng.wait_ge(self.sem, self.n)

    def step(self, ins):
        self.add(ins)
        self.wait()

    def restart(self):
        self.wait()
        self.eng.sem_clear(self.sem)
        self.n = 0


class Visit:

    def __init__(self, first, base=None, table=None):
        self.first, self.base, self.table = first, base, table
        self.slot = first % U
        self.par = first % 2

    def __add__(self, d):
        return Visit(self.first + d, self.base, self.table)

    @property
    def num(self):
        return self.first if self.base is None else self.base + self.first

    def round(self, per):
        if self.base is None:
            return per * (self.first // U + 1)
        return self.base * (per // U) + per * (self.first // U + 1)

    def chunk(self, eng):
        if self.table is None:
            return self.num // NT
        return eng.value_load(self.table[0:1, 0, bass.ds(self.num, 1)], min_val=0, max_val=NCH - 1)

    def node_tile(self, eng):
        if self.table is None:
            return self.num % NT
        return eng.value_load(self.table[0:1, 1, bass.ds(self.num, 1)], min_val=0, max_val=NT - 1)

    def num_past(self, n):
        return self.base is not None or self.first >= n

    def reused(self):
        return self.base is not None or self.first >= U


VG = NCH * NT
assert VG % U == 0


def program(nc, a, out):
    ctx = ExitStack()
    with ctx:
        def sb(name, shape, dt=F32):
            return ctx.enter_context(nc.sbuf_tensor(name, shape, dt))

        def ps(name, shape):
            return ctx.enter_context(nc.psum_tensor(name, shape, F32))

        def sem(name):
            return ctx.enter_context(nc.semaphore(name))

        src_tab = nc.dram_tensor("src_tab", [NP, D], F32)
        hid_tab = nc.dram_tensor("hid_tab", [NP, D], F32)
        vis_tab = nc.dram_tensor("vis_tab", [2, U * P], I32)

        ident = sb("ident", [P, P])
        iota = sb("iota", [P, P])
        nodecon = sb("nodecon", [P, NT, 2])
        vcol = sb("vcol", [P, U])
        ones = sb("ones", [1, P])
        w_edge0 = sb("w_edge0", [80, M0])
        w_ms0 = sb("w_ms0", [96, 160])
        w_mv0 = sb("w_mv0", [P, 2, P])
        w_hs0 = sb("w_hs0", [96, S])
        w_hv0 = sb("w_hv0", [P, 2, P])
        w2s = sb("w2s", [96, 1])
        w2v = sb("w2v", [P, 2])
        ws_val_t = sb("ws_val_t", [S, 96])
        wg = sb("wg", [S, C])
        adot = sb("adot", [P, S])
        gam_s = sb("gam_s", [S, 1])
        bet_s = sb("bet_s", [S, 1])
        gam_v = sb("gam_v", [96, 1])
        n0s = sb("n0s", [S, 2 * S])
        n0v = sb("n0v", [96, 192])
        e0s = sb("e0s", [S, S])
        e0v = sb("e0v", [96, 96])
        n1s = sb("n1s", [S, 160])
        n1v = sb("n1v", [96, 192])
        fc1 = sb("fc1", [64, P])
        w_edge1 = sb("w_edge1", [P, MW])
        l2s = sb("l2s", [96, 96])
        l2v = sb("l2v", [P, C])
        attr = sb("attr", [P, NT])

        X = sb("X", [P, NT, D])
        HN = sb("HN", [P, NT, D])
        TAB = sb("TAB", [P, NT, D])
        SC = sb("SC", [P, NT, 192])
        XN = SC[:, :, :].rearrange("p j f -> p (j f)")[:, 0:NT * D].rearrange("p (j f) -> p j f", j=NT)
        ACC = sb("ACC", [P, NT, MW])
        m_run = sb("m_run", [P, NT, H])
        st = sb("st", [P, 6, NT])
        accA = ACC[:, :, :].rearrange("p j f -> p (j f)")[:, 0:NT * H * HW].rearrange("p (j f) -> p j f", j=NT)
        DT = ACC[:, :, :].rearrange("p j f -> p (j f)")[:, NT * H * HW:NT * (H * HW + D)]\
            .rearrange("p (j f) -> p j f", j=NT)
        tr_n = sb("tr_n", [P, 4, P])
        o_n = sb("o_n", [P, 192])

        r0 = HN[0:1, :, :].rearrange("p j f -> p (j f)")
        last, lastf, tplus = (r0[:, (2 + i) * 800:(2 + i) * 800 + NCH] for i in range(3))
        last = last.bitcast(I32)
        spare = SC[:, :, :].rearrange("p j f -> p (j f)")[:, NT * D:NT * 192]
        bound, cmpv = spare[:, 0:NCH], spare[:, NCH:2 * NCH]
        tcol = sb("tcol", [P, 2, U])
        tcoli = sb("tcoli", [P, 2, U], I32)
        flag = sb("flag", [1, 1], I32)
        dstw = TAB[:, :, :].rearrange("p j f -> p (j f)")[:, 0:EP // P + 1].bitcast(I32)
        down = HN[:, :, :].rearrange("p j f -> p (j f)")[:, 0:EP // P + 1]
        onec = sb("onec", [P, 1])
        vis = sb("vis", [1, 2, U * P], I32)

        pack = sb("pack", [P, U, 6 * G], I32)
        sd = pack[:, :, 0:2 * G]
        yed = pack[:, :, 2 * G:6 * G].bitcast(F32)
        sdf = sb("sdf", [P, U, G])
        drow = sb("drow", [P, U, CH], I32)
        yrep = sb("yrep", [P, U, 2, CH])
        rrep = sb("rrep", [64, U, CH])
        zt = sb("zt", [80, U, CH])
        gat = sb("gat", [P, U, G * D])
        ohT = sb("ohT", [P, U, CH])
        ohE = sb("ohE", [P, U, G, P])
        mneg = sb("mneg", [P, U, CH])
        SV = sb("SV", [P, G, D + 64])
        M = sb("M", [P, 2, G, MW])
        row_n = M[:, 0, 0, :]
        tA = sb("tA", [P, G, 3, C])
        tB = sb("tB", [P, G, 3, C])
        tC = sb("tC", [P, G, 3, C])
        tD = sb("tD", [P, G, C])
        MT = sb("MT", [P, 4, G, P])
        MT2 = sb("MT2", [P, 4, G, P])
        M2 = sb("M2", [P, G, M0])
        th = sb("th", [P, 2, G, 96])
        sig = sb("sig", [P, G, 96])
        V2 = sb("V2", [P, G, 96 + 64])
        vv = sb("vv", [P, G, 96])
        tE = sb("tE", [P, G, 96])
        tF = sb("tF", [P, G, 96])
        tG = sb("tG", [P, G, 96])
        hv = sb("hv", [P, G, H, 24])
        lk = sb("lk", [P, G, S])
        lk2 = sb("lk2", [P, G, S])
        a4 = sb("a4", [P, U, G, H])
        scr = sb("scr", [P, CH])
        mo = sb("mo", [P, U, H])
        mn = sb("mn", [P, U, H])
        mdf = sb("mdf", [P, U, H])
        cor = sb("cor", [P, U, H])
        ad = sb("ad", [P, G * H])
        ex = sb("ex", [P, G * H])
        HX = sb("HX", [P, G, H, HW])
        atmp = sb("atmp", [P, H, HW])
        hid = MT2[:, 0:2].rearrange("p a g e -> p a (g e)")
        hidy = MT[:, :].rearrange("p (a b) g e -> p a b (g e)", a=2)

        W = ps("W", [P, G, 512])
        TR = ps("TR", [P, 8, P])
        DM = ps("DM", [P, 512])
        E1 = ps("E1", [P, G, 512])
        HP = ps("HP", [P, 512])
        AG0 = DM[:, G * D:G * D + H * HW]
        HV = HP[:, G * (S + H):G * (S + H + P)].rearrange("p (g f) -> p g f", g=G)
        AG = HP
        W_1 = TR[:, :, :].rearrange("p a b -> p (a b)").rearrange("p (g f) -> p g f", g=G)
        Wr = [W, W_1]

        s_const = sem("s_const")
        s_zero = sem("s_zero")
        s_w = sem("s_w")
        s_prep = sem("s_prep")
        s_wsg = sem("s_wsg")
        s_bnd = sem("s_bnd")
        s_tcol = sem("s_tcol")
        s_vst = sem("s_vst")
        s_vis = sem("s_vis")
        s_passed = sem("s_passed")
        s_dve = sem("s_dve")
        s_pool = sem("s_pool")
        s_act = sem("s_act")
        s_nrm = [sem(f"s_nrm{i}") for i in range(5)]
        s_sq = sem("s_sq")
        s_tab0 = sem("s_tab0")
        s_tab0d = sem("s_tab0d")
        s_tab1 = sem("s_tab1")
        s_tab1d = sem("s_tab1d")
        s_out = sem("s_out")
        s_outd = sem("s_outd")
        nd = {ph: {k: sem(f"{ph}_{k}") for k in ("row", "tr", "cp", "mm", "ev")} for ph in ("n0", "e0", "n1", "fi")}

        def node_tiles(eng, body):
            body(0, True)
            with eng.Fori(1, NT) as j:
                body(j, False)

        def node_pe(pe, ph, feats, mats):
            s = nd[ph]

            def body(j, first):
                if not first:
                    pe.wait_ge(s["cp"], j)
                pe.wait_ge(s["row"], j + 1)
                for b, (lo, w) in enumerate(feats):
                    ins = nc.tensor.transpose(TR[0:w, b, :], row_n[:, lo:lo + w], ident[:, :])
                ins.then_inc(s["tr"], 1)
                pe.wait_ge(s["cp"], j + 1)
                if not first:
                    pe.wait_ge(s["ev"], j)
                for o, lhs, rhs in mats:
                    ins = nc.tensor.matmul(o, lhs, rhs, start=True, stop=True)
                ins.then_inc(s["mm"], 1)
            node_tiles(pe, body)

        def node_act(act, ph, rows, width):
            def body(j, first):
                if not first:
                    act.wait_ge(nd[ph]["tr"], j)
                nc.scalar.activation(row_n[:, 0:width], rows[:, bass.ds(j, 1), :].rearrange("p a f -> p (a f)"),
                                     ACT.Copy).then_inc(nd[ph]["row"], 1)
            node_tiles(act, body)

        def loop_visits(eng, lead, tail, stage, finish=lambda total: None):
            def run(total, table):
                for t in range(-lead, U):
                    stage(Visit(t, None, table), total)
                with eng.Fori(U, total - U, U) as base:
                    for u in range(U):
                        stage(Visit(u, base, table), None)
                for t in range(total - U, total + tail):
                    stage(Visit(t, None, table), total)
                finish(total)

            descents = eng.value_load(flag[0:1, 0:1], min_val=0, max_val=EP)
            with eng.If(descents == 0):
                run(VS, vis)
            with eng.Else():
                run(VG, None)

        def inside(v, total):
            return total is None or 0 <= v.first < total

        LA = dict(ld=[sem(f"a_ld{u}") for u in range(U)], ga=[sem(f"a_ga{u}") for u in range(U)],
                  **{k: sem(f"a_{k}") for k in ("cvt", "z", "oh", "oht", "pre", "msg", "dup", "m", "t1", "c1", "e1", "th", "a4", "ab",
                                     "vg", "dup2", "cr", "m2c", "m2", "mx", "hxr", "t2", "c2", "h", "d", "ex", "hx", "exs", "sc", "acc")})
        LB = dict(ld=[sem(f"b_ld{u}") for u in range(U)], ga=[sem(f"b_ga{u}") for u in range(U)],
                  **{k: sem(f"b_{k}") for k in ("cvt", "oh", "fc", "hid", "hy", "w", "dup", "m", "sc", "acc")})

        def products(dve, ch, SVt, w_s0, w_sv, w_vs, w_dot, w_cr, Mt, dup_wait):
            nc.vector.tensor_tensor(Mt[:, :, 0:S], SVt[:, :, 0:S], w_s0, ALU.mult)
            v3 = SVt[:, :, S:D].rearrange("p g (k c) -> p g k c", k=3)
            blocks = Mt[:, :, 96:MW].rearrange("p g (k f) -> p g k f", k=3)
            for g in range(G):
                nc.vector.tensor_tensor(blocks[:, g, :, 0:S], ax(SVt[:, g, 0:S], (0, 3), (1, S)), w_sv(g), ALU.mult)
                nc.vector.tensor_tensor(blocks[:, g, :, S:S + C], v3[:, g], w_vs(g), ALU.mult)
                ch.add(nc.vector.tensor_tensor(tA[:, g], v3[:, g], w_dot(g), ALU.mult))
            dup_wait()
            for g in range(G):
                v5 = SVt[:, g, S:D + 64].rearrange("p (k c) -> p k c", k=5)
                nc.vector.tensor_tensor(tB[:, g], v5[:, 2:5], w_cr(g), ALU.mult)
                ch.add(nc.vector.tensor_tensor(tC[:, g], v5[:, 1:4], w_cr(g), ALU.mult))
            ch.wait()
            ch.add(nc.vector.tensor_tensor(tD[:, :, :], tA[:, :, 0], tA[:, :, 1], ALU.add))
            for k in range(3):
                nc.vector.tensor_tensor(blocks[:, :, k, S + C:], tB[:, :, (k + 2) % 3], tC[:, :, (k + 1) % 3],
                                        ALU.subtract)
            ch.wait()
            return nc.vector.tensor_tensor(Mt[:, :, S:96], tD[:, :, :], tA[:, :, 2], ALU.add)

        def k3(t):
            return t.rearrange("p g (k c) -> p g k c", k=3)

        def y_of(v, k, *dims):
            return ax(yed[:, v.slot, k:k + 1], (4, G), *dims)

        def norm(dve, ch, xin, lo, w, groups, mean_over, var_over, centre, s_centred, s_squared, dst, relu):
            cols = slice(lo, lo + w)
            if centre:
                ch.step(nc.vector.tensor_reduce(st[:, 0, :], xin[:, :, cols], AX.X, ALU.add))
                ch.step(nc.vector.tensor_scalar(st[:, 1, :], st[:, 0, :], 1.0 / mean_over, None, ALU.mult))
                ch.step(nc.vector.tensor_tensor(dst[:, :, cols], xin[:, :, cols],
                                                ax(st[:, 1, :], (1, NT), (0, w)), ALU.subtract))
                base = dst
            else:
                base = xin
            ch.step(nc.vector.tensor_tensor(TAB[:, :, cols], base[:, :, cols], base[:, :, cols], ALU.mult))
            ch.step(nc.vector.tensor_reduce(st[:, 2, :], TAB[:, :, cols], AX.X, ALU.add))
            ch.step(nc.vector.tensor_scalar(st[:, 3, :], st[:, 2, :], 1.0 / var_over, EPS, ALU.mult, ALU.add))
            nc.vector.tensor_copy(st[:, 4, :], st[:, 3, :]).then_inc(s_centred, 1)
            dve.wait_ge(s_squared, 1)
            ch.step(nc.vector.reciprocal(st[:, 5, :], st[:, 0, :]))
            ch.step(nc.vector.tensor_tensor(dst[:, :, cols], base[:, :, cols],
                                            ax(st[:, 5, :], (1, NT), (0, w)), ALU.mult))
            if relu:
                ch.step(nc.vector.tensor_scalar(dst[:, :, cols], dst[:, :, cols], 0.0, None, ALU.max))

        s_nc = [sem(f"s_nc{i}") for i in range(4)]
        s_ns = [sem(f"s_ns{i}") for i in range(4)]

        block = ctx.enter_context(nc.Block())

        n_const = [0]
        @block.sync
        def _(sp):
            n = 0

            def load(dst, src):
                nonlocal n
                sp.dma_start(dst, src).then_inc(s_const, 16)
                n += 1

            def rows(v):
                return v.rearrange("(f a) -> f a", a=1)
            load(X[:, :, :], a["x"].rearrange("(j p) f -> p j f", p=P))
            load(ident[:, :], a["c_ident"])
            load(iota[:, :], a["c_iota"])
            load(nodecon[:, :, :], a["c_nodecon"])
            load(vcol[:, :], a["c_vcol"])
            load(tplus[:, :], a["c_tplus"])
            load(last[:, :], a["last"])
            load(dstw, bass.AP(a["drow"].tensor, 0, [[EP // P, P], [1, EP // P + 1]]))
            load(attr[:, :], a["attr"])
            load(w_ms0[:, 0:64], a["W_alpha"])
            load(w_ms0[:, 96:160], a["Ws_val"])
            load(w_hs0[:, :], a["Ws_vlin"])
            load(w2s[0:64, :], rows(a["w2_ss"]))
            load(w2s[64:96, :], rows(a["w2_vv0"]))
            for k in range(3):
                load(w2v[C * k:C * (k + 1), 0:1], rows(a["w2_vs"]))
                load(w2v[C * k:C * (k + 1), 1:2], rows(a["w2_vv1"]))
            for b in range(2):
                load(w2v[96:128, b:b + 1], rows(a["w2_sv"])[C * b:C * (b + 1), :])
            load(ws_val_t[:, :], a["Ws_val_T"])
            load(wg[:, :], a["Wg"])
            load(adot[:, :], a["adot_rep"])
            load(gam_s[:, :], rows(a["gamma_s"]))
            load(bet_s[:, :], rows(a["beta_s"]))
            load(n0s[:, 0:S], a["Ws_src"])
            load(n0s[:, S:2 * S], a["Ws_dst"])
            load(e0s[:, :], a["Wps"])
            load(n1s[:, 0:96], a["sc_ws"])
            load(n1s[:, 96:160], a["lin1_ws"])
            load(fc1[:, 0:64], a["fc_w1"])
            load(fc1[:, 64:128], a["fc_w1"])
            load(l2s[:, :], a["lin2_ws"])
            load(l2v[:, :], a["lin2_wv"])
            sp.wait_ge(s_zero, 8)
            load(w_edge1[0:64, 0:64], a["fc_w2"][:, 0:64])
            load(w_edge1[0:64, 64:96], a["fc_w2"][:, 128:160])
            for k in range(3):
                rs, b = slice(64 * ((k + 1) % 2), 64 * ((k + 1) % 2) + 64), 96 + P * k
                load(w_edge1[rs, b:b + 64], a["fc_w2"][:, 64:128])
                load(w_edge1[rs, b + 64:b + 128], a["fc_w2"][:, 160:224])
            for k in range(3):
                r, c = slice(C * k, C * k + C), C * k
                load(gam_v[r, :], rows(a["gamma_v"]))
                load(n0v[r, c:c + C], a["Wv_src"])
                load(n0v[r, 96 + c:96 + c + C], a["Wv_dst"])
                load(e0v[r, c:c + C], a["Wpv"])
                load(n1v[r, c:c + C], a["sc_wv"])
                load(n1v[r, 96 + c:96 + c + C], a["lin1_wv"])
                rr = slice(16 * (k + 1), 16 * (k + 2))
                load(w_edge0[rr, 160 + c:160 + c + C], a["W_rbf"][:, 160:192])
                load(w_edge0[rr, 256 + c:256 + c + C], a["W_rbf"][:, 192:224])
                for w, m in ((w_mv0, a["Wv_val"]), (w_hv0, a["Wv_vlin"])):
                    load(w[r, 0, c:c + C], m[64:96, :])
                    load(w[r, 1, c:c + C], m[96:128, :])
            for w, m in ((w_mv0, a["Wv_val"]), (w_hv0, a["Wv_vlin"])):
                for b in range(2):
                    load(w[96:128, b, 96:128], m[C * b:C * (b + 1), :])
            load(w_edge0[64:80, 96:160], a["W_rbf"][:, 64:128])
            load(w_edge0[0:16, 0:64], a["W_rbf"][:, 0:64])
            load(w_edge0[0:16, 64:96], a["W_rbf"][:, 128:160])
            n_const[0] = n

            sp.wait_ge(s_tcol, 1)
            with nc.allow_non_contiguous_dma(reason="512 words once"):
                for r in range(2):
                    sp.dma_start(vis_tab.ap()[r, :].rearrange("(c p) -> p c", p=P), tcoli[:, r, :]).then_inc(s_vst, 16)
            sp.wait_ge(s_vst, 32)
            sp.dma_start(vis[:, :, :].rearrange("a r v -> a (r v)"),
                         vis_tab.ap().rearrange("(a r) v -> a (r v)", a=1)).then_inc(s_vis, 16)
            sp.wait_ge(s_vis, 16)
            sp.wait_ge(s_tab0, 1)
            sp.dma_start(src_tab.ap().rearrange("(j p) f -> p j f", p=P), TAB[:, :, :]).then_inc(s_tab0d, 16)

            def chunk_rows(t, T, *dims):
                row = t[0:1, bass.ds(T, 1), :]
                return bass.AP(row.tensor, row.offset, [list(d) for d in dims] + [[1, CH]])

            def visit_loads(v, total, L, free, extra):
                if not inside(v, total):
                    return
                T = v.chunk(sp)
                if v.reused():
                    for name in free:
                        sp.wait_ge(L[name], v.num - (U - 1))
                s = v.slot
                sp.dma_start(pack[:, s, :], a["pack"][bass.ds(T, 1)].rearrange("t p c -> (t p) c")).then_inc(L["ld"][s], 16)
                extra(T, s)

            def extra0(T, s):
                row = a["drow"][bass.ds(T, 1), :]
                sp.dma_start(drow[:, s, :], row.to_broadcast([P, CH])).then_inc(LA["ld"][s], 16)
                sp.dma_start(yrep[0:64, s, 0, :], chunk_rows(a["yT"], T, (EP, 4), (0, 16))).then_inc(LA["ld"][s], 16)
                sp.dma_start(rrep[:, s, :], chunk_rows(a["rbfT"], T, (0, 4), (EP, 16))).then_inc(LA["ld"][s], 16)
                sp.dma_start(zt[64:80, s, :], chunk_rows(a["rbfT"], T, (EP, 16))).then_inc(LA["ld"][s], 16)

            def extra1(T, s):
                for kk in range(2):
                    yr = a["yT"][2 * kk:2 * kk + 1, bass.ds(T, 1), :]
                    yr = bass.AP(yr.tensor, yr.offset, [[EP, 2], [0, 64], [1, CH]])
                    sp.dma_start(yrep[:, s, kk, :], yr).then_inc(LB["ld"][s], 16)
                sp.dma_start(rrep[:, s, :], chunk_rows(a["e64T"], T, (EP, 64))).then_inc(LB["ld"][s], 16)

            loop_visits(sp, 0, 0, lambda v, total: visit_loads(v, total, LA, ("hx",), extra0))

            sp.wait_ge(s_tab1, 1)
            sp.dma_start(hid_tab.ap().rearrange("(j p) f -> p j f", p=P), TAB[:, :, :]).then_inc(s_tab1d, 16)
            loop_visits(sp, 0, 0, lambda v, total: visit_loads(v, total, LB, ("oh", "hy", "dup"), extra1))

            sp.wait_ge(s_out, 1)
            sp.dma_start(out.rearrange("(j p) f -> p j f", p=P), X[:, :, :]).then_inc(s_outd, 16)
            sp.wait_ge(s_outd, 16)
            sp.wait_ge(s_tab0d, 16)
            sp.wait_ge(s_tab1d, 16)

        n_loads = n_const[0]

        @block.gpsimd
        def _(pool):
            ch = Chain(pool, s_pool)
            nc.gpsimd.memset(ones[:, :], 1.0)
            for t in (gam_v[:, :], n0v[:, :], e0v[:, :], n1v[:, :], w_edge0[:, :], w_edge1[:, :], w_mv0[:, :, :],
                      w_hv0[:, :, :]):
                nc.gpsimd.memset(t, 0.0).then_inc(s_zero, 1)
            nc.gpsimd.memset(m_run[:, :, :], NEG)
            nc.gpsimd.memset(ACC[:, :, :], 0.0).then_inc(s_prep, 1)
            pool.wait_ge(s_vis, 16)
            pool.wait_ge(s_tab0d, 16)

            def wait(sem, count):
                pool.wait_ge(sem, count)
                pool.sem_inc(s_passed, 1)

            def gathers(v, L, tab, nld):
                s = v.slot
                wait(L["ld"][s], v.round(16 * nld))
                for g in range(G):
                    pool.indirect_dma_start(gat[:, s, g * D:(g + 1) * D], None, tab.ap(),
                                            bass.IndirectOffsetOnAxis(ap=sd[:, s, g:g + 1], axis=0))\
                        .then_inc(L["ga"][s], 16)

            def stage0(v, total):
                if not inside(v, total):
                    return
                s = v.slot
                gathers(v, LA, src_tab, 5)
                nc.gpsimd.tensor_copy(sdf[:, s, :], sd[:, s, G:2 * G])
                nc.gpsimd.tensor_tensor(zt[0:64, s, :], rrep[:, s, :], yrep[0:64, s, 0, :], ALU.mult)\
                    .then_inc(LA["z"], 1)

            def cross2(v, total):
                if not inside(v, total):
                    return
                y3 = y_of(v, 1, (1, 3), (0, C))
                wait(LA["dup2"], v.num + 1)
                nc.gpsimd.tensor_tensor(k3(tE[:, :, :]), k3(V2[:, :, 64:160]), y3, ALU.mult)
                nc.gpsimd.tensor_tensor(k3(tF[:, :, :]), k3(V2[:, :, 32:128]), y3, ALU.mult).then_inc(LA["cr"], 1)
                wait(LA["cr"], v.num + 1)
                if v.num_past(1):
                    wait(LA["t2"], v.num)
                for k in range(3):
                    i, j = C * ((k + 2) % 3), C * ((k + 1) % 3)
                    ins = nc.gpsimd.tensor_tensor(M2[:, :, 224 + C * k:224 + C * (k + 1)], tE[:, :, i:i + C],
                                                  tF[:, :, j:j + C], ALU.subtract)
                ins.then_inc(LA["m2c"], 1)

            def pool0(t, total):
                cross2(t + -1, total)
                stage0(t + 2, total)
            loop_visits(pool, 2, 1, pool0)
            pool.wait_ge(s_nrm[0], 1)
            nc.gpsimd.memset(ACC[:, :, :], 0.0).then_inc(s_prep, 1)
            pool.wait_ge(s_tab1d, 16)

            def stage1(v, total):
                if not inside(v, total):
                    return
                if v.num_past(U):
                    wait(LB["dup"], v.num - (U - 1))
                    wait(LB["sc"], v.num - (U - 1))
                gathers(v, LB, hid_tab, 4)
                nc.gpsimd.tensor_copy(sdf[:, v.slot, :], sd[:, v.slot, G:2 * G]).then_inc(LB["cvt"], 1)
            loop_visits(pool, 0, 0, stage1)

        @block.tensor
        def _(pe):
            pe.wait_ge(s_const, 16 * n_loads)
            nc.tensor.matmul(DM[0:96, 0:C], ws_val_t[:, :], wg[:, :], start=True, stop=True).then_inc(s_wsg, 1)
            pe.wait_ge(s_bnd, 2)
            pe.wait_ge(s_prep, 1)
            nc.tensor.matmul(HP[0:1, 0:1], down[:, EP // P:EP // P + 1], onec[:, :], start=True, stop=True)\
                .then_inc(s_wsg, 1)
            nc.tensor.matmul(E1[:, 0, 0:NCH], ones[:, :], lastf[:, :],
                             start=True, stop=True).then_inc(s_wsg, 1)

            pe.wait_ge(s_nrm[1], 1)
            node_pe(pe, "n0", [(S, 96), (0, S)], [
                (ax(DM[:, 0:1], (D, 2), (1, S)), tr_n[0:S, 1, :], n0s[:, :].rearrange("p (a f) -> p a f", a=2)),
                (ax(DM[:, S:S + 1], (D, 2), (1, 96)), tr_n[0:96, 0, :], n0v[:, :].rearrange("p (a f) -> p a f", a=2))])

            def pre0(v, total):
                if not inside(v, total):
                    return
                s = v.slot
                J = v.node_tile(pe)
                pe.wait_ge(LA["z"], v.num + 1)
                pe.wait_ge(LA["oh"], v.num + 1)
                if v.num_past(1):
                    pe.wait_ge(LA["m"], v.num)
                for g in range(G):
                    es = slice(g * P, g * P + P)
                    nc.tensor.matmul(W[:, g, 0:M0], zt[:, s, es], w_edge0[:, :], start=True, stop=True)
                    ins = nc.tensor.matmul(DM[:, g * D:(g + 1) * D], ohT[:, s, es],
                                           DT[:, bass.ds(J, 1), :].rearrange("p a f -> p (a f)"),
                                           start=True, stop=True)
                ins.then_inc(LA["pre"], 1)

            def turn(Mt, sem_done):
                for b, (lo, w) in enumerate(B0):
                    for g in range(G):
                        ins = nc.tensor.transpose(TR[0:w, b * G + g, :], Mt[:, g, lo:lo + w], ident[:, :])
                ins.then_inc(sem_done, 1)

            def t1(v, total):
                if not inside(v, total):
                    return
                pe.wait_ge(LA["m"], v.num + 1)
                if v.num_past(2):
                    pe.wait_ge(LA["c2"], v.num - 1)
                turn(M[:, 0], LA["t1"])

            def e1(v, total):
                if not inside(v, total):
                    return
                pe.wait_ge(LA["c1"], v.num + 1)
                if v.num_past(1):
                    pe.wait_ge(LA["mx"], v.num)
                for g in range(G):
                    nc.tensor.matmul(E1[:, g, 0:160], MT[0:96, 0, g, :], w_ms0[:, :], start=True, stop=True)
                    for b in range(2):
                        ins = nc.tensor.matmul(E1[:, g, 160:160 + P], MT[:, 1 + b, g, :], w_mv0[:, b, :],
                                               start=(b == 0), stop=(b == 1))
                ins.then_inc(LA["e1"], 1)

            def ab(v, total):
                if not inside(v, total):
                    return
                pe.wait_ge(LA["a4"], v.num + 1)
                pe.wait_ge(LA["th"], v.num + 1)
                for h in range(H):
                    for g in range(G):
                        ins = nc.tensor.transpose(E1[:, h // 2, (h % 2 * G + g) * P:(h % 2 * G + g + 1) * P],
                                                  ax(a4[:, v.slot, g, h:h + 1], (0, P)), ident[:, :])
                ins.then_inc(LA["ab"], 1)

            def t2(v, total):
                if not inside(v, total):
                    return
                pe.wait_ge(LA["m2"], v.num + 1)
                pe.wait_ge(LA["m2c"], v.num + 1)
                if total is None or v.first + 1 < total:
                    pe.wait_ge(LA["c1"], v.num + 2)
                turn(M2, LA["t2"])

            def hm(v, total):
                if not inside(v, total):
                    return
                pe.wait_ge(LA["c2"], v.num + 1)
                if v.num_past(1):
                    pe.wait_ge(LA["hx"], v.num)
                pe.wait_ge(LA["mx"], v.num + 1)
                for g in range(G):
                    nc.tensor.matmul(HP[:, g * S:(g + 1) * S], MT2[0:96, 0, g, :], w_hs0[:, :], start=True, stop=True)
                    for b in range(2):
                        nc.tensor.matmul(HV[:, g, :], MT2[:, 1 + b, g, :], w_hv0[:, b, :], start=(b == 0), stop=(b == 1))
                    ins = nc.tensor.matmul(HP[:, G * S + g * H:G * S + (g + 1) * H], ohT[:, v.slot, g * P:(g + 1) * P],
                                           mn[:, v.slot, :], start=True, stop=True)
                ins.then_inc(LA["h"], 1)

            def sc0(v, total):
                if not inside(v, total):
                    return
                pe.wait_ge(LA["hx"], v.num + 1)
                pe.wait_ge(LA["exs"], v.num + 1)
                if v.num_past(1):
                    pe.wait_ge(LA["acc"], v.num)
                for g in range(G):
                    ins = nc.tensor.matmul(AG0, ohE[:, v.slot, g, :],
                                           HX[:, g].rearrange("p h f -> p (h f)"), start=(g == 0), stop=(g == G - 1))
                ins.then_inc(LA["sc"], 1)

            def stage0(t, total):
                t2(t + -2, total)
                ab(t + -1, total)
                hm(t + -2, total)
                t1(t, total)
                pre0(t + 1, total)
                sc0(t + -2, total)
                e1(t, total)
            pe.wait_ge(s_prep, 3)
            pe.wait_ge(s_tab0, 1)
            pe.wait_ge(s_vis, 16)
            loop_visits(pe, 1, 2, stage0)

            pe.wait_ge(s_nrm[0], 1)
            node_pe(pe, "e0", [(S, 96), (0, S)], [
                (DM[:, 0:S], tr_n[0:S, 1, :], e0s[:, :]), (DM[:, S:D], tr_n[0:96, 0, :], e0v[:, :])])
            pe.wait_ge(s_nrm[2], 1)
            node_pe(pe, "n1", [(S, 96), (0, S)], [
                (DM[:, 0:160], tr_n[0:S, 1, :], n1s[:, :]), (DM[:, 160:352], tr_n[0:96, 0, :], n1v[:, :])])

            def fc(v, total):
                if not inside(v, total):
                    return
                pe.wait_ge(LB["ld"][v.slot], v.round(16 * 4))
                if v.num_past(1):
                    pe.wait_ge(LB["hid"], v.num)
                nc.tensor.matmul(DM[:, 0:CH], fc1[:, :], rrep[:, v.slot, :], start=True, stop=True).then_inc(LB["fc"], 1)

            def w1(v, total):
                if not inside(v, total):
                    return
                pe.wait_ge(LB["hy"], v.num + 1)
                if v.num_past(2):
                    pe.wait_ge(LB["m"], v.num - 1)
                for g in range(G):
                    for kk, (lo, w) in enumerate(((0, 96 + P), (96 + P, 2 * P))):
                        ins = nc.tensor.matmul(Wr[v.par][:, g, lo:lo + w], hidy[:, v.par, kk, g * P:(g + 1) * P],
                                               w_edge1[:, lo:lo + w], start=True, stop=True)
                ins.then_inc(LB["w"], 1)

            def sc1(v, total):
                if not inside(v, total):
                    return
                pe.wait_ge(LB["oh"], v.num + 1)
                pe.wait_ge(LB["m"], v.num + 1)
                if v.num_past(1):
                    pe.wait_ge(LB["acc"], v.num)
                for g in range(G):
                    ins = nc.tensor.matmul(AG[:, 0:MW], ohE[:, v.slot, g, :], M[:, v.par, g, :],
                                           start=(g == 0), stop=(g == G - 1))
                ins.then_inc(LB["sc"], 1)

            def stage1(t, total):
                w1(t + 1, total)
                fc(t + 3, total)
                sc1(t, total)
            pe.wait_ge(s_tab1, 1)
            loop_visits(pe, 3, 0, stage1)
            pe.wait_ge(s_nrm[3], 1)
            node_pe(pe, "fi", [(0, 96)] + [(96 + P * k, P) for k in range(3)], [
                (DM[:, 0:96], tr_n[0:96, 0, :], l2s[:, :])] + [
                (DM[:, 96 + C * k:96 + C * (k + 1)], tr_n[:, 1 + k, :], l2v[:, :]) for k in range(3)])

        @block.scalar
        def _(act):
            def root(i):
                act.wait_ge(s_nc[i], 1)
                nc.scalar.activation(st[:, 0, :], st[:, 4, :], ACT.Sqrt).then_inc(s_ns[i], 1)
            for i in range(3):
                root(i)
            act.wait_ge(s_nrm[1], 1)
            node_act(act, "n0", XN, D)

            def dup(v, total, L, wait_name, src, sem_done):
                if not inside(v, total):
                    return
                act.wait_ge(L[wait_name], v.num + 1)
                nc.scalar.activation(src[:, :, D:D + 64], src[:, :, S:S + 64], ACT.Copy).then_inc(L[sem_done], 1)

            def copies(v, total, turned, dst, sem_done, freed):
                if not inside(v, total):
                    return
                act.wait_ge(LA[turned], v.num + 1)
                if v.num_past(1):
                    act.wait_ge(LA[freed], v.num)
                nc.scalar.activation(dst[0:96, 0].rearrange("p g e -> p (g e)"),
                                     TR[0:96, 0:G, :].rearrange("p g e -> p (g e)"), ACT.Copy)
                nc.scalar.activation(dst[:, 1:3].rearrange("p k g e -> p (k g e)"),
                                     TR[:, G:3 * G, :].rearrange("p a e -> p (a e)"), ACT.Copy).then_inc(LA[sem_done], 1)

            def values2(v, total):
                if not inside(v, total):
                    return
                act.wait_ge(LA["vg"], v.num + 1)
                if v.num_past(1):
                    act.wait_ge(LA["t2"], v.num)
                    act.wait_ge(LA["cr"], v.num)
                nc.scalar.activation(V2[:, :, 96:160], V2[:, :, 0:64], ACT.Copy)
                nc.scalar.activation(ax(M2[:, 0, 192:193], (M0, G), (P, 2), (1, C)),
                                     ax(sig[:, 0, C:C + 1], (96, G), (C, 2), (1, C)), ACT.Copy).then_inc(LA["dup2"], 1)

            def tanh(v, total):
                if not inside(v, total):
                    return
                act.wait_ge(LA["e1"], v.num + 1)
                if v.num_past(2):
                    act.wait_ge(LA["vg"], v.num - 1)
                nc.scalar.activation(th[:, v.par], E1[:, :, 64:160], ACT.Tanh, scale=0.5).then_inc(LA["th"], 1)

            def exps(v, total):
                if not inside(v, total):
                    return
                act.wait_ge(LA["d"], v.num + 1)
                if v.num_past(1):
                    act.wait_ge(LA["hx"], v.num)
                    act.wait_ge(LA["sc"], v.num)
                nc.scalar.activation(cor[:, v.slot, :], mdf[:, v.slot, :], ACT.Exp)
                nc.scalar.activation(ex[:, :], ad[:, :], ACT.Exp).then_inc(LA["ex"], 1)
                act.wait_ge(LA["ex"], v.num + 1)
                nc.scalar.activation(ax(HX[:, 0, 0, HW - 1:HW], (HW, G * H)), ex[:, :], ACT.Copy)\
                    .then_inc(LA["exs"], 1)

            def stage0(t, total):
                copies(t + -2, total, "t2", MT2, "c2", "h")
                values2(t + -1, total)
                dup(t, total, LA, "msg", SV, "dup")
                copies(t, total, "t1", MT, "c1", "e1")
                exps(t + -2, total)
                tanh(t, total)
            loop_visits(act, 0, 2, stage0)
            act.wait_ge(s_nrm[0], 1)
            node_act(act, "e0", XN, D)
            root(3)
            act.wait_ge(s_nrm[2], 1)
            node_act(act, "n1", HN, D)

            def stage1(t, total):
                v = t + 3
                if inside(v, total):
                    act.wait_ge(LB["fc"], v.num + 1)
                    if v.num_past(2):
                        act.wait_ge(LB["hy"], v.num - 1)
                    nc.scalar.activation(hid[:, v.par, :], DM[:, 0:CH], ACT.Silu, scale=0.125).then_inc(LB["hid"], 1)
                v = t
                if inside(v, total):
                    act.wait_ge(LB["ga"][v.slot], v.round(16 * G))
                    if v.num_past(1):
                        act.wait_ge(LB["m"], v.num)
                    gv = gat[:, v.slot, :].rearrange("p (g f) -> p g f", g=G)
                    nc.scalar.activation(SV[:, :, 0:D], gv, ACT.Copy)
                    nc.scalar.activation(SV[:, :, D:D + 64], gv[:, :, S:S + 64], ACT.Copy).then_inc(LB["dup"], 1)
            loop_visits(act, 3, 0, stage1)
            act.wait_ge(s_nrm[3], 1)
            node_act(act, "fi", ACC, MW)

            act.wait_ge(s_nrm[4], 1)
            nc.scalar.activation(TAB[:, :, 0:64], SC[:, :, 0:64], ACT.Silu)
            nc.scalar.activation(TAB[:, :, 64:96], SC[:, :, 64:96], ACT.Sigmoid).then_inc(s_sq, 1)

        @block.vector
        def _(dve):
            ch = Chain(dve, s_dve)
            TT, TS = nc.vector.tensor_tensor, nc.vector.tensor_scalar
            fA, fB, fC = (t[:, :, :, :].rearrange("p g k c -> p g (k c)") for t in (tA, tB, tC))
            dve.wait_ge(s_const, 16 * n_loads)
            TS(w_edge0[:, 160:256], w_edge0[:, 160:256], R3, None, ALU.mult)
            TS(w_edge0[:, 256:352], w_edge0[:, 256:352], R2, None, ALU.mult)
            ws = 1.0 / (8.0 * 4.0)
            for lo, dims, f in ((0, [(1, 96)], ws), (96, [(P, 3), (1, 64)], ws), (160, [(P, 3), (1, C)], ws * R3),
                                (192, [(P, 3), (1, C)], ws * R2)):
                v = ax(w_edge1[:, lo:lo + 1], *dims)
                TS(v, v, f, None, ALU.mult)
            TS(w2s[64:96, :], w2s[64:96, :], R3, None, ALU.mult)
            ch.step(TS(w2v[0:96, 1:2], w2v[0:96, 1:2], R2, None, ALU.mult))
            TS(w_hs0[:, :], w_hs0[:, :], w2s[:, 0:1], None, ALU.mult)
            for b in range(2):
                TS(w_hv0[:, b, :], w_hv0[:, b, :], w2v[:, b:b + 1], None, ALU.mult)
            dve.wait_ge(s_wsg, 1)
            nc.vector.tensor_copy(w_ms0[:, 64:96], DM[0:96, 0:C])
            w = EP // P
            ch.step(TT(down[:, 0:w], dstw[:, 0:w], dstw[:, 1:w + 1], ALU.is_gt))
            ch.step(nc.vector.tensor_reduce(down[:, w:w + 1], down[:, 0:w], AX.X, ALU.max))
            nc.vector.memset(onec[:, :], 1.0).then_inc(s_bnd, 1)
            ch.step(nc.vector.tensor_single_scalar(last[:, :], last[:, :], 7, ALU.arith_shift_right))
            ch.step(nc.vector.tensor_copy(lastf[:, :], last[:, :]))
            TT(lastf[:, :], lastf[:, :], tplus[:, :], ALU.add).then_inc(s_bnd, 1)
            dve.wait_ge(s_wsg, 3)
            ch.step(nc.vector.tensor_copy(flag[:, :], HP[0:1, 0:1]))
            ch.step(nc.vector.tensor_copy(bound[:, :], E1[:, 0, 0:NCH]))
            for c in range(U):
                ch.step(TS(cmpv[:, :], bound[:, :], vcol[:, c:c + 1], None, ALU.is_le))
                ch.step(nc.vector.tensor_reduce(tcol[:, 0, c:c + 1], cmpv[:, :], AX.X, ALU.add))
            ch.step(TT(tcol[:, 1, :], vcol[:, :], tcol[:, 0, :], ALU.subtract))
            nc.vector.tensor_copy(tcoli[:, :, :], tcol[:, :, :]).then_inc(s_tcol, 1)

            norm(dve, ch, X, 0, D, 1, D, D, True, s_nc[0], s_ns[0], HN, True)
            norm(dve, ch, HN, 0, S, 1, S, S, True, s_nc[1], s_ns[1], XN, False)
            norm(dve, ch, HN, S, 96, 1, C, C, False, s_nc[2], s_ns[2], XN, False)
            dve.sem_inc(s_nrm[1], 1)

            def node_dve(ph, evac, out_done, copy_out):
                s = nd[ph]

                def body(j, first):
                    dve.wait_ge(s["tr"], j + 1)
                    copy_out().then_inc(s["cp"], 1)
                    dve.wait_ge(s["mm"], j + 1)
                    evac(j).then_inc(s["ev"], 1)
                node_tiles(dve, body)

            def scaled_copy():
                TS(tr_n[0:S, 1, :], TR[0:S, 1, :], gam_s[:, 0:1], bet_s[:, 0:1], ALU.mult, ALU.add)
                return TS(tr_n[0:96, 0, :], TR[0:96, 0, :], gam_v[:, 0:1], None, ALU.mult)

            def plain_copy():
                nc.vector.tensor_copy(tr_n[0:S, 1, :], TR[0:S, 1, :])
                return nc.vector.tensor_copy(tr_n[0:96, 0, :], TR[0:96, 0, :])

            def tile_of(t, j):
                return t[:, bass.ds(j, 1)].rearrange("p a f -> p (a f)")

            def evac_n0(j):
                nc.vector.tensor_copy(tile_of(TAB, j), DM[:, 0:D])
                return nc.vector.tensor_copy(tile_of(DT, j), DM[:, D:2 * D])
            dve.wait_ge(s_prep, 1)
            node_dve("n0", evac_n0, None, scaled_copy)
            dve.wait_ge(nd["n0"]["ev"], NT)
            dve.sem_inc(s_tab0, 1)
            dve.sem_inc(s_prep, 2)
            ch.wait()
            dve.wait_ge(s_vis, 16)

            def a_part(v, total):
                if not inside(v, total):
                    return
                s = v.slot
                dve.wait_ge(LA["ga"][s], v.round(16 * G))
                dve.wait_ge(LA["pre"], v.num + 1)
                gv = gat[:, s, :].rearrange("p (g f) -> p g f", g=G)
                TT(SV[:, :, 0:D], gv, DM[:, 0:G * D].rearrange("p (g f) -> p g f", g=G), ALU.add)\
                    .then_inc(LA["msg"], 1)
                dve.wait_ge(LA["msg"], v.num + 1)
                if v.num_past(1):
                    dve.wait_ge(LA["t1"], v.num)
                Mt, v5 = M[:, 0], SV[:, :, S:D + 64]
                TT(Mt[:, :, 0:S], SV[:, :, 0:S], W[:, :, 0:S], ALU.mult)
                TT(k3(Mt[:, :, 96:192]), k3(v5[:, :, 0:96]), ax(W[:, 0, 64:65], (512, G), (0, 3), (1, C)), ALU.mult)
                TT(ax(Mt[:, 0, 192:193], (MW, G), (P, 2), (1, C)), ax(SV[:, 0, 0:1], (D + 64, G), (C, 2), (1, C)),
                   ax(W[:, 0, 96:97], (512, G), (C, 2), (1, C)), ALU.mult)
                TT(fA, v5[:, :, 0:96], W[:, :, 160:256], ALU.mult)
                dve.wait_ge(LA["dup"], v.num + 1)
                TT(fB, v5[:, :, 64:160], W[:, :, 256:352], ALU.mult)
                ch.step(TT(fC, v5[:, :, 32:128], W[:, :, 256:352], ALU.mult))
                ch.add(TT(tD[:, :, :], fA[:, :, 0:C], fA[:, :, C:2 * C], ALU.add))
                for k in range(3):
                    i, j = C * ((k + 2) % 3), C * ((k + 1) % 3)
                    TT(Mt[:, :, 224 + C * k:224 + C * (k + 1)], fB[:, :, i:i + C], fC[:, :, j:j + C], ALU.subtract)
                ch.wait()
                TT(Mt[:, :, S:96], tD[:, :, :], fA[:, :, 2 * C:96], ALU.add).then_inc(LA["m"], 1)

            def one_hots(v, total):
                if not inside(v, total):
                    return
                s = v.slot
                J = v.node_tile(dve)
                dve.wait_ge(LA["z"], v.num + 1)
                if v.num_past(U):
                    dve.wait_ge(LA["sc"], v.num - (U - 1))
                one_hot_edges(s, J)
                ch.step(TS(ohT[:, s, :], drow[:, s, :], nodecon[:, bass.ds(J, 1), 0:1].rearrange("p a f -> p (a f)"),
                           None, ALU.is_equal))
                TS(mneg[:, s, :], ohT[:, s, :], 1.0, -NEG, ALU.subtract, ALU.mult).then_inc(LA["oh"], 1)

            def one_hot_edges(s, J):
                for g in range(G):
                    ins = TS(ohE[:, s, g, :], iota[:, :], sdf[:, s, g:g + 1],
                             nodecon[:, bass.ds(J, 1), 1:2].rearrange("p a f -> p (a f)"), ALU.subtract, ALU.is_equal)
                return ins

            def hx_part(v, total):
                if not inside(v, total):
                    return
                s = v.slot
                dve.wait_ge(LA["h"], v.num + 1)
                ch.step(TT(ad[:, :], a4[:, s].rearrange("p g h -> p (g h)"), HP[:, G * S:G * S + G * H], ALU.subtract))
                TS(ad[:, :], ad[:, :], 0.0, None, ALU.min).then_inc(LA["d"], 1)
                ch.step(TT(k3(tG[:, :, :]), ax(HV[:, 0, 96:97], (P, G), (0, 3), (1, C)), y_of(v, 1, (1, 3), (0, C)), ALU.mult))
                for g in range(G):
                    ins = TT(ax(hv[:, g, 0, 0:1], (8, 3), (24, H), (1, 8)), ax(HV[:, g, 0:1], (C, 3), (8, H), (1, 8)),
                             ax(tG[:, g, 0:1], (C, 3), (8, H), (1, 8)), ALU.add)
                ch.step(ins)
                dve.wait_ge(LA["ex"], v.num + 1)
                if v.num_past(1):
                    dve.wait_ge(LA["sc"], v.num)
                TT(ax(HX[:, 0, 0, 0:1], (HW, G * H), (1, 16)), ax(HP[:, 0:1], (16, G * H), (1, 16)),
                   ax(ex[:, 0:1], (1, G * H), (0, 16)), ALU.mult)
                TT(ax(HX[:, 0, 0, 16:17], (HW, G * H), (1, 24)), ax(hv[:, 0, 0, 0:1], (24, G * H), (1, 24)),
                   ax(ex[:, 0:1], (1, G * H), (0, 24)), ALU.mult).then_inc(LA["hx"], 1)

            def b1_part(v, total):
                if not inside(v, total):
                    return
                s = v.slot
                dve.wait_ge(LA["th"], v.num + 1)
                if v.num_past(1):
                    dve.wait_ge(LA["cr"], v.num)
                    dve.wait_ge(LA["m2"], v.num)
                TS(sig[:, :, :], th[:, v.par], 0.5, 0.5, ALU.mult, ALU.add)
                TT(k3(fA), ax(E1[:, 0, 256:257], (512, G), (0, 3), (1, C)), y_of(v, 1, (1, 3), (0, C)), ALU.mult)
                ch.step(TS(lk[:, :, :], E1[:, :, 0:S], 0.2, None, ALU.mult))
                TT(lk2[:, :, :], E1[:, :, 0:S], lk[:, :, :], ALU.max)
                ch.step(TT(vv[:, :, :], E1[:, :, 160:256], fA, ALU.add))
                TT(k3(V2[:, :, 0:96]), k3(vv[:, :, :]), ax(sig[:, 0, 0:1], (96, G), (0, 3), (1, C)), ALU.mult)\
                    .then_inc(LA["vg"], 1)
                ch.step(TT(lk[:, :, :], lk2[:, :, :], ax(adot[:, 0:1], (0, G), (1, S)), ALU.mult))
                nc.vector.tensor_reduce(a4[:, s].rearrange("p g h -> p (g h)"),
                                        ax(lk[:, 0, 0:1], (16, G * H), (1, 16)), AX.X, ALU.add).then_inc(LA["a4"], 1)

            def acc_part(v, total):
                if not inside(v, total):
                    return
                J = v.node_tile(dve)
                tj = accA[:, bass.ds(J, 1), :].rearrange("p a f -> p (a f)")
                if v.num_past(1):
                    dve.wait_ge(LA["acc"], v.num)
                ch.step(TT(atmp[:, :, :], tj.rearrange("p (h f) -> p h f", h=H),
                           ax(cor[:, v.slot, 0:1], (1, H), (0, HW)), ALU.mult))
                dve.wait_ge(LA["sc"], v.num + 1)
                TT(tj, atmp[:, :, :].rearrange("p h f -> p (h f)"), AG0, ALU.add).then_inc(LA["acc"], 1)

            def m2_part(v, total):
                if not inside(v, total):
                    return
                dve.wait_ge(LA["vg"], v.num + 1)
                if v.num_past(1):
                    dve.wait_ge(LA["t2"], v.num)
                TT(M2[:, :, 0:S], sig[:, :, C:96], y_of(v, 0, (0, S)), ALU.mult)
                TT(M2[:, :, 96:192], V2[:, :, 0:96], y_of(v, 0, (0, 96)), ALU.mult)
                ch.step(TT(k3(fA), k3(V2[:, :, 0:96]), y_of(v, 1, (1, 3), (0, C)), ALU.mult))
                ch.step(TT(tD[:, :, :], fA[:, :, 0:C], fA[:, :, C:2 * C], ALU.add))
                TT(M2[:, :, S:96], tD[:, :, :], fA[:, :, 2 * C:96], ALU.add).then_inc(LA["m2"], 1)

            def mx_part(v, total):
                if not inside(v, total):
                    return
                s = v.slot
                J = v.node_tile(dve)
                mj = m_run[:, bass.ds(J, 1), :].rearrange("p a f -> p (a f)")
                ch.step(nc.vector.tensor_copy(mo[:, s, :], mj))
                dve.wait_ge(LA["ab"], v.num + 1)
                for h in range(H):
                    ch.step(nc.vector.tensor_tensor_reduce(
                        out=scr[:, :], in0=E1[:, h // 2, h % 2 * CH:(h % 2 + 1) * CH], in1=mneg[:, s, :],
                        scale=1.0, scalar=mo[:, s, h:h + 1], op0=ALU.add, op1=ALU.max, accum_out=mn[:, s, h:h + 1]))
                nc.vector.tensor_copy(mj, mn[:, s, :])
                TT(mdf[:, s, :], mo[:, s, :], mn[:, s, :], ALU.subtract).then_inc(LA["mx"], 1)

            def stage0(t, total):
                ch.restart()
                acc_part(t + -3, total)
                one_hots(t + 1, total)
                b1_part(t + -1, total)
                a_part(t, total)
                mx_part(t + -1, total)
                hx_part(t + -2, total)
                m2_part(t + -1, total)
            loop_visits(dve, 1, 3, stage0, lambda total: dve.wait_ge(LA["acc"], total))

            ch.restart()
            aj = accA.rearrange("p j (h f) -> p j h f", h=H)
            den = XN[:, :, 0:H]
            rec = TAB[:, :, 0:H]
            dve.wait_ge(s_tab0d, 16)
            ch.step(TS(den, aj[:, :, :, HW - 1], 1e-16, None, ALU.add))
            ch.step(nc.vector.reciprocal(rec, den))
            for h in range(H):
                r = ax(TAB[:, 0, h:h + 1], (D, NT), (0, 16))
                TT(XN[:, :, 16 * h:16 * h + 16], aj[:, :, h, 0:16], r, ALU.mult)
                for k in range(3):
                    r = ax(TAB[:, 0, h:h + 1], (D, NT), (0, 8))
                    lo = S + C * k + 8 * h
                    ins = TT(XN[:, :, lo:lo + 8], aj[:, :, h, 16 + 8 * k:24 + 8 * k], r, ALU.mult)
            ch.step(ins)
            dve.sem_inc(s_nrm[0], 1)
            ch.step(TT(X[:, :, :], X[:, :, :], HN[:, :, :], ALU.add))

            def evac_e0(j):
                return TT(tile_of(X, j), tile_of(X, j), DM[:, 0:D], ALU.add)
            node_dve("e0", evac_e0, None, plain_copy)
            dve.wait_ge(nd["e0"]["ev"], NT)
            norm(dve, ch, X, 0, D, 1, D, D, True, s_nc[3], s_ns[3], HN, True)
            dve.sem_inc(s_nrm[2], 1)

            def evac_n1(j):
                nc.vector.tensor_copy(tile_of(SC, j)[:, 0:96], DM[:, 0:96])
                nc.vector.tensor_copy(tile_of(SC, j)[:, 96:192], DM[:, 160:256])
                nc.vector.tensor_copy(tile_of(TAB, j)[:, 0:S], DM[:, 96:160])
                return nc.vector.tensor_copy(tile_of(TAB, j)[:, S:D], DM[:, 256:352])
            node_dve("n1", evac_n1, None, plain_copy)
            dve.wait_ge(nd["n1"]["ev"], NT)
            cs, cv = S ** -0.5, C ** -0.5
            ch.step(TT(TAB[:, :, :], TAB[:, :, :], ax(attr[:, 0:1], (1, NT), (0, D)), ALU.mult))
            TS(TAB[:, :, 0:S], TAB[:, :, 0:S], cs, None, ALU.mult)
            ch.step(TS(TAB[:, :, S:D], TAB[:, :, S:D], cv, None, ALU.mult))
            dve.sem_inc(s_tab1, 1)
            dve.wait_ge(s_prep, 4)

            def one_hots1(v, total):
                if not inside(v, total):
                    return
                J = v.node_tile(dve)
                dve.wait_ge(LB["cvt"], v.num + 1)
                if v.num_past(U):
                    dve.wait_ge(LB["sc"], v.num - (U - 1))
                one_hot_edges(v.slot, J).then_inc(LB["oh"], 1)

            def hy(v, total):
                if not inside(v, total):
                    return
                dve.wait_ge(LB["hid"], v.num + 1)
                if v.num_past(2):
                    dve.wait_ge(LB["w"], v.num - 1)
                for kk in range(2):
                    ins = TT(hidy[:, v.par, kk, :], hid[:, v.par, :], yrep[:, v.slot, kk, :], ALU.mult)
                ins.then_inc(LB["hy"], 1)

            def m_part(v, total):
                if not inside(v, total):
                    return
                dve.wait_ge(LB["dup"], v.num + 1)
                dve.wait_ge(LB["w"], v.num + 1)
                if v.num_past(2):
                    dve.wait_ge(LB["sc"], v.num - 1)
                w = Wr[v.par]
                products(dve, ch, SV, w[:, :, 0:S],
                         lambda g: ax(w[:, g, 96:97], (P, 3), (1, S)),
                         lambda g: ax(w[:, g, 64:65], (0, 3), (1, C)),
                         lambda g: ax(w[:, g, 160:161], (P, 3), (1, C)),
                         lambda g: ax(w[:, g, 192:193], (P, 3), (1, C)),
                         M[:, v.par], lambda: None).then_inc(LB["m"], 1)

            def acc1(v, total):
                if not inside(v, total):
                    return
                J = v.node_tile(dve)
                dve.wait_ge(LB["sc"], v.num + 1)
                if v.num_past(1):
                    dve.wait_ge(LB["acc"], v.num)
                TT(tile_of(ACC, J), tile_of(ACC, J), AG[:, 0:MW], ALU.add).then_inc(LB["acc"], 1)

            def stage1(t, total):
                ch.restart()
                m_part(t, total)
                hy(t + 2, total)
                one_hots1(t + 1, total)
                acc1(t + -1, total)
            loop_visits(dve, 2, 1, stage1, lambda total: dve.wait_ge(LB["acc"], total))
            ch.restart()
            TS(SC[:, :, 0:96], SC[:, :, 0:96], cs, None, ALU.mult)
            ch.step(TS(SC[:, :, 96:192], SC[:, :, 96:192], cv, None, ALU.mult))
            dve.sem_inc(s_nrm[3], 1)

            def four_copies():
                nc.vector.tensor_copy(tr_n[0:96, 0, :], TR[0:96, 0, :])
                return nc.vector.tensor_copy(tr_n[:, 1:4, :], TR[:, 1:4, :])

            def evac_fi(j):
                TS(o_n[:, 0:96], DM[:, 0:96], 96.0 ** -0.5, None, ALU.mult)
                ch.add(TS(o_n[:, 96:192], DM[:, 96:192], 128.0 ** -0.5, None, ALU.mult))
                ch.wait()
                ins = TT(tile_of(SC, j), tile_of(SC, j), o_n[:, :], ALU.add)
                return ins
            s = nd["fi"]

            def body(j, first):
                ch.restart()
                dve.wait_ge(s["tr"], j + 1)
                four_copies().then_inc(s["cp"], 1)
                dve.wait_ge(s["mm"], j + 1)
                if not first:
                    dve.wait_ge(s["ev"], j)
                evac_fi(j).then_inc(s["ev"], 1)
            node_tiles(dve, body)
            dve.wait_ge(s["ev"], NT)
            ch.restart()
            ch.step(TT(SC[:, :, :], SC[:, :, :], ax(attr[:, 0:1], (1, NT), (0, 192)), ALU.mult))
            dve.wait_ge(s_tab1d, 16)
            dve.sem_inc(s_nrm[4], 1)
            dve.wait_ge(s_sq, 1)
            for k in range(3):
                ins = TT(SC[:, :, 96 + C * k:96 + C * (k + 1)], SC[:, :, 96 + C * k:96 + C * (k + 1)],
                         TAB[:, :, 64:96], ALU.mult)
            ch.step(ins)
            TT(X[:, :, 0:S], X[:, :, 0:S], TAB[:, :, 0:S], ALU.add)
            ch.step(TT(X[:, :, S:D], X[:, :, S:D], SC[:, :, 96:192], ALU.add))
            dve.sem_inc(s_out, 1)


def _columns():
    return np.concatenate([np.arange(S)] + [S + 3 * np.arange(C) + k for k in range(3)])


def kernel(**inputs):
    import concourse.bacc as bacc
    from concourse.bass_utils import run_bass_kernel_spmd

    g = {k: np.ascontiguousarray(v) for k, v in inputs.items()}
    perm = _columns()

    def chunks(v, pad):
        full = np.full((EP,) + v.shape[1:], pad, v.dtype)
        full[:E] = v
        return full

    src, dst = chunks(g["src"].astype(np.int32), 0), chunks(g["dst"].astype(np.int32), NP - 1)
    y, rbf, e64 = chunks(g["edge_attr_4"], 0), chunks(g["edge_attr_16"], 0), chunks(g["edge_attr_64"], 0)
    x = np.zeros((NP, D), np.float32)
    x[:N] = g["x"][:, perm]
    attr = np.zeros((NP, 1), np.float32)
    attr[:N] = g["node_vec1"]
    tile = lambda v: np.ascontiguousarray(v.reshape(NCH, G, P, -1).transpose(0, 2, 1, 3))
    arr = {
        "x": x, "attr": attr.reshape(NT, P).T,
        "pack": np.concatenate([tile(src)[..., 0], tile(dst)[..., 0],
                                tile(y).reshape(NCH, P, G * 4).view(np.int32)], -1),
        "drow": np.concatenate([dst, np.full(CH, NP - 1, np.int32)]).reshape(NCH + 1, CH),
        "last": dst.reshape(NCH, CH)[:, CH - 1][None],
        "yT": y.T.reshape(4, NCH, CH),
        "rbfT": rbf.T.reshape(16, NCH, CH),
        "e64T": e64.T.reshape(64, NCH, CH),
        "Ws_val_T": g["L0_gnn_Ws_val"].T,
        "adot_rep": np.broadcast_to(g["L0_gnn_alpha_dot"].reshape(1, S), (P, S)),
        "c_ident": np.eye(P, dtype=np.float32),
        "c_iota": np.broadcast_to(np.arange(P, dtype=np.float32), (P, P)),
        "c_nodecon": np.stack([np.arange(P)[:, None] + P * np.arange(NT)[None],
                               np.broadcast_to(-P * np.arange(NT), (P, NT))], -1).astype(np.float32),
        "c_vcol": (np.arange(P)[:, None] + P * np.arange(U)[None]).astype(np.float32),
        "c_tplus": np.arange(1, NCH + 1, dtype=np.float32)[None],
    }
    for k, v in g.items():
        if k.startswith("L0_gnn_") or k.startswith("L1_gnn_"):
            arr[k[7:]] = v
    arr = {k: np.ascontiguousarray(v) for k, v in arr.items()}
    nc = bacc.Bacc("TRN2", target_bir_lowering=False, num_devices=1)
    aps = {k: nc.dram_tensor("in_" + k, v.shape, mybir.dt.from_np(v.dtype), kind="ExternalInput").ap()
           for k, v in arr.items()}
    out = nc.dram_tensor("out_x", (NP, D), F32, kind="ExternalOutput").ap()
    program(nc, aps, out)
    r = run_bass_kernel_spmd(nc, [{"in_" + k: v for k, v in arr.items()}], core_ids=[0])
    res = r.results[0]["out_x"][:N]
    full = np.empty_like(res)
    full[:, perm] = res
    return full
```
